# Optimizing a Trainium2 kernel written in Bass

```python
import numpy as np
import jax
import jax.numpy as jnp

def _softmax(x, axis=-1):
    return jax.nn.softmax(x, axis=axis)

def _gelu(x):
    return jax.nn.gelu(x, approximate=True)

def _silu(x):
    return jax.nn.silu(x)

def _sigmoid(x):
    return jax.nn.sigmoid(x)

def _layernorm(x, axis=-1, eps=1e-05):
    m = jnp.mean(x, axis=axis, keepdims=True)
    v = jnp.var(x, axis=axis, keepdims=True)
    return (x - m) / jnp.sqrt(v + eps)

def _scatter_add(tgt, idx, src, axis=0):
    return tgt.at[idx].add(src)

def _segment_sum(src, seg, n):
    return jax.ops.segment_sum(src, seg, n)
kernel_name = 'mk_xattn_ffn_d1_seqx_r4_7d3f17'

def setup_inputs(seed: int=0):
    np.random.seed(seed)
    _w = jnp.asarray

    def _rec_inputs():
        import jax
        import jax.numpy as jnp
        _rk = jax.random.key(seed)
        x = -0.0005207 + 1.001 * jax.random.normal(jax.random.fold_in(_rk, 1), (2, 512, 1024), jnp.float32)
        _lenS = 512 - jax.random.randint(jax.random.fold_in(_rk, 7), (2,), 0, max(1, 512 // 4) + 1, jnp.int32)
        _lenS2 = 1024 - jax.random.randint(jax.random.fold_in(_rk, 8), (2,), 0, max(1, 1024 // 4) + 1, jnp.int32)
        _ctx_4096P = jax.random.normal(jax.random.fold_in(_rk, 11), (2, 16, 1024), jnp.float32)
        _ctx_4096c = jax.random.dirichlet(jax.random.fold_in(_rk, 511), 0.3 * jnp.ones((16,), jnp.float32), (2, 1024))
        _ctx_4096t = jnp.einsum('bsk,bkd->bsd', _ctx_4096c, _ctx_4096P)
        _ctx_4096t = _ctx_4096t * jax.lax.rsqrt(jnp.mean(jnp.square(_ctx_4096t)) + 1e-12) * 0.953939
        ctx_4096 = -0.00010331 + 0.999899 * (_ctx_4096t + 0.3 * jax.random.normal(jax.random.fold_in(_rk, 611), (2, 1024, 1024), jnp.float32))
        return (x, ctx_4096)
    x, ctx_4096 = _rec_inputs()

    def _L0_xattn_setup():
        import jax, jax.numpy as jnp
        import numpy as np
        HEADS = 32
        KV_HEADS = 8
        HEAD_DIM = 128
        EPS = 1e-06

        def rms_norm(x, w):
            var = jnp.mean(jnp.square(x.astype(jnp.float32)), axis=-1, keepdims=True)
            return (x.astype(jnp.float32) * jax.lax.rsqrt(var + EPS)).astype(x.dtype) * w
        key = jax.random.key(seed)
        ks = jax.random.split(key, 6)
        bsz, n_lat, seq, hidden = (8, 64, 1024, 1024)
        return {'latents': jax.random.normal(ks[0], (bsz, n_lat, hidden), jnp.float32), 'context': jax.random.normal(ks[1], (bsz, seq, hidden), jnp.float32), 'Wq': jax.random.normal(ks[2], (hidden, HEADS * HEAD_DIM), jnp.float32) * 0.02, 'Wk': jax.random.normal(ks[3], (hidden, KV_HEADS * HEAD_DIM), jnp.float32) * 0.02, 'Wv': jax.random.normal(ks[4], (hidden, KV_HEADS * HEAD_DIM), jnp.float32) * 0.02, 'Wo': jax.random.normal(ks[5], (HEADS * HEAD_DIM, hidden), jnp.float32) * 0.02, 'q_norm_w': jnp.ones((HEAD_DIM,), jnp.float32), 'k_norm_w': jnp.ones((HEAD_DIM,), jnp.float32)}
    _L0_xattn_all = _L0_xattn_setup()
    _L0_xattn_in = {k: v for k, v in _L0_xattn_all.items() if k in ('Wq', 'Wk', 'Wv', 'Wo', 'q_norm_w', 'k_norm_w')}
    del _L0_xattn_all

    def _L0_ffn_setup():
        import jax, jax.numpy as jnp
        import numpy as np
        BATCH, SEQ, D = (2, 512, 1024)
        K, TOPK, RANK = (64, 16, 16)
        ALPHA = 32.0
        SCALING = ALPHA / RANK
        key = jax.random.key(seed)
        k1, k2, k3, k4 = jax.random.split(key, 4)
        x = jax.random.normal(k1, (BATCH, SEQ, D), dtype=jnp.float32)
        A = jax.random.normal(k2, (K, RANK, D), dtype=jnp.float32) * 0.02
        B = jax.random.normal(k3, (K, D, RANK), dtype=jnp.float32) * 0.02
        Wr = jax.random.normal(k4, (K, D), dtype=jnp.float32) * 0.02
        return {'x': x, 'A': A, 'B': B, 'Wr': Wr}
    _L0_ffn_all = _L0_ffn_setup()
    _L0_ffn_in = {k: v for k, v in _L0_ffn_all.items() if k in ('A', 'B', 'Wr')}
    del _L0_ffn_all
    return {'x': x, 'ctx_4096': ctx_4096, 'L0_xattn_Wq': _L0_xattn_in['Wq'], 'L0_xattn_Wk': _L0_xattn_in['Wk'], 'L0_xattn_Wv': _L0_xattn_in['Wv'], 'L0_xattn_Wo': _L0_xattn_in['Wo'], 'L0_xattn_q_norm_w': _L0_xattn_in['q_norm_w'], 'L0_xattn_k_norm_w': _L0_xattn_in['k_norm_w'], 'L0_ffn_A': _L0_ffn_in['A'], 'L0_ffn_B': _L0_ffn_in['B'], 'L0_ffn_Wr': _L0_ffn_in['Wr']}

def reference(x, ctx_4096, L0_xattn_Wq, L0_xattn_Wk, L0_xattn_Wv, L0_xattn_Wo, L0_xattn_q_norm_w, L0_xattn_k_norm_w, L0_ffn_A, L0_ffn_B, L0_ffn_Wr):
    import jax
    import jax.numpy as jnp

    def _L0_xattn_ref(latents, context, Wq, Wk, Wv, Wo, q_norm_w, k_norm_w):
        import jax, jax.numpy as jnp
        import numpy as np
        HEADS = 32
        KV_HEADS = 8
        HEAD_DIM = 128
        EPS = 1e-06

        def rms_norm(x, w):
            var = jnp.mean(jnp.square(x.astype(jnp.float32)), axis=-1, keepdims=True)
            return (x.astype(jnp.float32) * jax.lax.rsqrt(var + EPS)).astype(x.dtype) * w
        bsz, q_len, hidden = latents.shape
        kv = jnp.concatenate([context, latents], axis=1)
        kv_len = kv.shape[1]
        groups = HEADS // KV_HEADS
        q = (latents @ Wq).reshape(bsz, q_len, HEADS, HEAD_DIM).transpose(0, 2, 1, 3)
        k = (kv @ Wk).reshape(bsz, kv_len, KV_HEADS, HEAD_DIM).transpose(0, 2, 1, 3)
        v = (kv @ Wv).reshape(bsz, kv_len, KV_HEADS, HEAD_DIM).transpose(0, 2, 1, 3)
        q = rms_norm(q, q_norm_w)
        k = rms_norm(k, k_norm_w)
        qg = q.reshape(bsz, KV_HEADS, groups, q_len, HEAD_DIM)
        scale = 1.0 / np.sqrt(HEAD_DIM)
        scores = jnp.einsum('bhgqd,bhkd->bhgqk', qg, k) * scale
        probs = jax.nn.softmax(scores.astype(jnp.float32), axis=-1).astype(q.dtype)
        out = jnp.einsum('bhgqk,bhkd->bhgqd', probs, v)
        out = out.reshape(bsz, HEADS, q_len, HEAD_DIM).transpose(0, 2, 1, 3)
        out = out.reshape(bsz, q_len, HEADS * HEAD_DIM)
        return out @ Wo

    def _L0_ffn_ref(x, A, B, Wr):
        import jax, jax.numpy as jnp
        import numpy as np
        BATCH, SEQ, D = (2, 512, 1024)
        K, TOPK, RANK = (64, 16, 16)
        ALPHA = 32.0
        SCALING = ALPHA / RANK
        prefix = x.shape[:-1]
        xf = x.reshape(-1, x.shape[-1])
        N = xf.shape[0]
        scores = xf @ Wr.T
        top_vals, top_idx = jax.lax.top_k(scores, TOPK)
        gates = jax.nn.softmax(top_vals, axis=-1)
        G = jnp.zeros((N, K), xf.dtype).at[jnp.arange(N)[:, None], top_idx].set(gates)
        h = jnp.einsum('nd,krd->nkr', xf, A)
        out = jnp.einsum('nkr,kdr->nd', h * G[:, :, None], B)
        return (out * SCALING).reshape(*prefix, -1)
    x = x + _L0_xattn_ref(_layernorm(x, axis=-1), ctx_4096, L0_xattn_Wq, L0_xattn_Wk, L0_xattn_Wv, L0_xattn_Wo, L0_xattn_q_norm_w, L0_xattn_k_norm_w)
    x = x + _L0_ffn_ref(_layernorm(x, axis=-1), L0_ffn_A, L0_ffn_B, L0_ffn_Wr)
    return x

_drawn_inputs = setup_inputs


def setup_inputs(seed=0):
    import zlib

    import numpy as np

    out = dict(_drawn_inputs(seed))
    spreads = {'L0_xattn_q_norm_w': (1.0, 0.6), 'L0_xattn_k_norm_w': (1.0, 0.6)}
    factors = {}
    for name, (base, spread) in spreads.items():
        noise = np.random.default_rng([zlib.crc32(name.encode()), seed]).standard_normal(out[name].shape)
        drawn = base * np.exp(spread * noise) if base else spread * noise
        out[name] = jnp.asarray(drawn.astype(out[name].dtype))
    for name, factor in factors.items():
        out[name] = (out[name] * factor).astype(out[name].dtype)
    return out
```

```python
import concourse.bass as bass
from concourse import mybir
from contextlib import ExitStack

F32 = mybir.dt.float32
F32R = mybir.dt.float32r
ACT = mybir.ActivationFunctionType
ALU = mybir.AluOpType
AX = mybir.AxisListType

P = 128
NB = 2
SQ = 512
SC = 1024
SK = SC + SQ
D = 1024
DC = D // P
HEADS = 32
KVH = 8
DH = 128
GRP = HEADS // KVH
QT = SQ // P
KT = SK // P
CW = 512
HPC = CW // DH
LN_EPS = 1e-5
RMS_EPS = 1e-6
EXPERTS = 64
RANK = 16
KR = EXPERTS * RANK
GATE_SCALE = 32.0 / RANK


def split_matmul(nc, out, w_hi, w_lo, x_hi, x_lo, start, stop):
    nc.tensor.matmul(out, w_hi, x_hi, start=start, stop=False)
    nc.tensor.matmul(out, w_hi, x_lo, start=False, stop=False)
    return nc.tensor.matmul(out, w_lo, x_hi, start=False, stop=stop)


def projections(nc, x, ctx_t, w_kvq, q_norm, k_norm, ident, k_s, v_s, q_s):
    NKV = KVH // HPC
    NQC = HEADS // HPC
    CTX_PIECE = 256
    PIECE = DC * CTX_PIECE
    WROWS = PIECE // CW
    WP = DC // WROWS
    CP = SC // CTX_PIECE
    UNITS = 2 * NKV * KT + NQC * QT
    NORMS = NKV * KT + NQC * QT
    VUNITS = NKV * KT
    ITEMS = CP + WP * (2 * NKV + NQC)
    K_UNITS = NKV * KT
    LAST = UNITS - 1

    with ExitStack() as ctx:
        def sb(name, shape, dt=F32):
            return ctx.enter_context(nc.sbuf_tensor(name, shape, dt))

        def sem(name):
            return ctx.enter_context(nc.semaphore(name))

        kv_hi = sb("kv_hi", [P, DC, SK], F32R)
        kv_lo = sb("kv_lo", [P, DC, SK], F32R)
        w_hi = sb("w_hi", [P, 2, DC, CW], F32R)
        w_lo = sb("w_lo", [P, 2, DC, CW], F32R)
        stage = sb("stage_a", [P, 2, PIECE])
        xt = sb("xt_a", [P, 2, D])
        sq = sb("sq", [P, 2, CW])
        kn = sb("kn", [P, 2, CW])
        ev = sb("ev", [P, 2, CW])
        vev = sb("vev", [P, 2, CW])
        ln_st = sb("ln_st_a", [P, 2, 2, 6])
        ln_mv = sb("ln_mv_a", [P, 2, 2])
        ln_r = sb("ln_r_a", [P, 2, 2])
        ss = sb("ss", [P, 2, 3, HPC])
        wn = sb("wn", [P, 2])
        wqs = sb("wqs", [P, 1])
        ps_u = ctx.enter_context(nc.psum_tensor("ps_u", [P, 4, CW], F32))
        ps_t = ctx.enter_context(nc.psum_tensor("ps_t", [P, 2, CW], F32))
        ps_x = ctx.enter_context(nc.psum_tensor("ps_x", [P, 2, CW], F32))

        s_stage = [sem("a_stage0"), sem("a_stage1")]
        s_hi = sem("a_hi")
        s_lo = sem("a_lo")
        s_x = [sem("a_x0"), sem("a_x1")]
        s_w = sem("a_w")
        s_wqs = sem("a_wqs")
        s_carry = sem("a_carry")
        s_id = sem("a_id")
        s_unit = sem("a_unit")
        s_sq = sem("a_sq")
        s_dv = sem("a_dv")
        s_var = sem("a_var")
        s_sqrt = sem("a_sqrt")
        s_kn = sem("a_kn")
        s_tr = sem("a_tr")
        s_ev = sem("a_ev")
        s_vev = sem("a_vev")
        s_st = [sem("a_st0"), sem("a_st1")]
        s_vst = [sem("a_vst0"), sem("a_vst1")]
        s_lnv = sem("a_lnv")
        s_lnq = sem("a_lnq")
        s_xn = sem("a_xn")
        s_xtr = sem("a_xtr")
        s_xhi = sem("a_xhi")
        s_xlo = sem("a_xlo")
        block = ctx.enter_context(nc.Block())

        w_view = w_kvq.rearrange("(j p) n -> p j n", p=P)

        head_items = [("w", 0, 0), ("c", 0, 0), ("w", 0, 1), ("c", 0, 1), ("c", 0, 2), ("c", 0, 3)]
        head_items += [("w", ci, p) for ci in range(1, 2 * NKV) for p in range(WP)]
        W_READY = {0: 3, 1: CP + 2 * WP, 2: CP + 3 * WP, 3: CP + 4 * WP}
        C_READY = [2, 4, 5, 6]
        SHARED = 3

        def split_target(kind, ci, p):
            if kind == "w":
                rows = slice(p * WROWS, (p + 1) * WROWS)
                return w_hi[:, ci % 2, rows, :], w_lo[:, ci % 2, rows, :]
            cols = slice(p * CTX_PIECE, (p + 1) * CTX_PIECE)
            return kv_hi[:, :, cols], kv_lo[:, :, cols]

        @block.sync
        def _(sp):
            def load(item, free, src):
                sp.wait_ge(s_lo, free)
                sp.dma_start(stage[:, item % 2, :].rearrange("p (j n) -> p j n", j=src.shape[1]),
                             src).then_inc(s_stage[item % 2], 16)

            with sp.Fori(0, NB) as b:
                ctx_b = ctx_t[bass.ds(b, 1), :, :].rearrange("o (j p) t -> p (o j) t", p=P)
                for i, (kind, ci, p) in enumerate(head_items):
                    if kind == "w":
                        src = w_view[:, p * WROWS:(p + 1) * WROWS, ci * CW:(ci + 1) * CW]
                    else:
                        src = ctx_b[:, :, p * CTX_PIECE:(p + 1) * CTX_PIECE]
                    load(i, b * ITEMS + ITEMS + i - 1, src)
                    if i == SHARED - 1:
                        for t in range(2):
                            sp.wait_ge(s_xtr, b * 2 * QT + 2 * QT)
                            sp.dma_start(xt[:, t, :], x[bass.ds(b * SQ + t * P, P), :]).then_inc(s_x[t], 16)
                    if i == 5:
                        for t in range(2, QT):
                            sp.wait_ge(s_xtr, b * 2 * QT + 2 * QT + 2 * (t - 1))
                            sp.dma_start(xt[:, t % 2, :], x[bass.ds(b * SQ + t * P, P), :]).then_inc(s_x[t % 2], 16)
                with sp.Fori(0, NQC // 2) as j:
                    for c in range(2):
                        for p in range(WP):
                            i = len(head_items) + c * WP + p
                            load(i, b * ITEMS + j * (2 * WP) + (ITEMS + i - 1),
                                 w_view[:, p * WROWS:(p + 1) * WROWS, bass.ds(j * (2 * CW) + (2 * NKV + c) * CW, CW)])

        @block.gpsimd
        def _(pool):
            pool.sem_inc(s_lo, ITEMS)
            nc.gpsimd.memset(ident[:, :], 0.0).then_inc(s_id, 1)
            pool.wait_ge(s_id, 1)
            nc.gpsimd.affine_select(out=ident[:, :], in_=ident[:, :], compare_op=ALU.not_equal, fill=1.0, base=0,
                                    pattern=[[-1, P]], channel_multiplier=1).then_inc(s_id, 1)

            def split(item, ready, done, free, hi, lo):
                raw = stage[:, item % 2, :].rearrange("p (j n) -> p j n", j=hi.shape[1])
                pool.wait_ge(s_stage[item % 2], ready)
                pool.wait_ge(s_unit, free)
                pool.sem_inc(s_carry, 1)
                nc.gpsimd.tensor_scalar(hi, raw, 1.0, 1.0, ALU.mult, ALU.mult).then_inc(s_hi, 1)
                pool.wait_ge(s_hi, done)
                nc.gpsimd.tensor_tensor(lo, raw, hi.bitcast(F32), ALU.subtract).then_inc(s_lo, 1)

            def batch(b, first):
                for i, (kind, ci, p) in enumerate(head_items):
                    if first and i < SHARED:
                        continue
                    hi, lo = split_target(kind, ci, p)
                    if kind == "w":
                        free = (-QT, 0, KT, 2 * KT)[ci]
                    else:
                        free = -NQC * QT
                    split(i, b * (8 * ITEMS) + 16 * (i // 2 + 1), b * ITEMS + i + 1,
                          b * UNITS + UNITS + free, hi, lo)
                with pool.Fori(0, NQC // 2) as j:
                    for c in range(2):
                        for p in range(WP):
                            i = len(head_items) + c * WP + p
                            rows = slice(p * WROWS, (p + 1) * WROWS)
                            split(i, b * (8 * ITEMS) + j * (16 * WP) + 16 * (i // 2 + 1),
                                  b * ITEMS + j * (2 * WP) + i + 1,
                                  b * UNITS + j * (2 * QT) + (UNITS + 4 * KT - (QT if c == 0 else 0)),
                                  w_hi[:, c, rows, :], w_lo[:, c, rows, :])

            pool.wait_ge(s_lo, ITEMS + SHARED)
            batch(0, True)
            with pool.Fori(1, NB) as b:
                batch(b, False)

        def unit_plan():
            return ([("k", c, t) for c in range(NKV) for t in range(KT)]
                    + [("v", NKV + c, t) for c in range(NKV) for t in range(KT)])

        PLAN = unit_plan()

        @block.tensor
        def _(pe):
            pe.sem_inc(s_unit, UNITS)
            pe.sem_inc(s_xtr, 2 * QT)
            pe.sem_inc(s_tr, NORMS)
            pe.wait_ge(s_id, 2)

            def product(u, wbuf, t, rest_ready=None):
                cols = slice(t * P, (t + 1) * P)
                for j in range(DC):
                    if rest_ready is not None and j == WROWS:
                        pe.wait_ge(s_lo, rest_ready)
                    last = split_matmul(nc, ps_u[:, u % 4, :], kv_hi[:, j, cols], kv_lo[:, j, cols],
                                        w_hi[:, wbuf, j, :], w_lo[:, wbuf, j, :], j == 0, j == DC - 1)
                last.then_inc(s_unit, 1)

            def transposes(m, ready, free):
                pe.wait_ge(s_kn, ready)
                pe.wait_ge(s_ev, free)
                for h in range(HPC):
                    last = nc.tensor.transpose(ps_t[:, m % 2, h * P:(h + 1) * P], kn[:, m % 2, h * P:(h + 1) * P],
                                               ident[:, :])
                last.then_inc(s_tr, 1)

            with pe.Fori(0, NB) as b:
                for u, (kind, ci, t) in enumerate(PLAN):
                    if t == 0 and u > 0:
                        pe.wait_ge(s_lo, b * ITEMS + ITEMS + W_READY[ci])
                    if u % 2 == 0 and u < 2 * CP:
                        pe.wait_ge(s_lo, b * ITEMS + ITEMS + C_READY[u // 2])
                    if u == 2 * CP:
                        pe.wait_ge(s_xlo, b * 2 * QT + 4 * QT)
                    if u < K_UNITS + 4:
                        pe.wait_ge(s_kn, b * NORMS + NORMS + u - 3)
                    else:
                        pe.wait_ge(s_vev, b * VUNITS + (u - K_UNITS - 3))
                    product(u, ci % 2, t, b * ITEMS + ITEMS + W_READY[0] if u == 0 else None)
                    if 2 <= u < 2 + QT:
                        for e in range(2):
                            n = 2 * (u - 2) + e
                            pe.wait_ge(s_xn, b * QT + u - 1)
                            pe.wait_ge(s_xlo, b * 2 * QT + (n + 2 * QT - 1))
                            for j in range(HPC):
                                last = nc.tensor.transpose(
                                    ps_x[:, e, j * P:(j + 1) * P],
                                    xt[:, (u - 2) % 2, (e * HPC + j) * P:(e * HPC + j + 1) * P], ident[:, :])
                            last.then_inc(s_xtr, 1)
                    if 1 <= u <= K_UNITS:
                        m = u - 1
                        transposes(m, b * NORMS + NORMS + m + 1, b * NORMS + NORMS + m - 1)

                def q_pass(j):
                    for c in range(2):
                        for t in range(QT):
                            r = c * QT + t
                            if t == 0:
                                pe.wait_ge(s_lo, b * ITEMS + j * (2 * WP) + ITEMS + CP + (2 * NKV + c + 1) * WP)
                            m = K_UNITS + r
                            if r < 4:
                                pe.wait_ge(s_vev, b * VUNITS + VUNITS)
                            pe.wait_ge(s_kn, b * NORMS + j * (2 * QT) + (NORMS + m - 3))
                            product(r, c, (KT - QT) + t)
                            if r >= 1 or not isinstance(j, int):
                                transposes(m - 1, b * NORMS + j * (2 * QT) + (NORMS + m),
                                           b * NORMS + j * (2 * QT) + (NORMS + m - 2))

                q_pass(0)
                with pe.Fori(1, NQC // 2) as j:
                    q_pass(j)
                transposes(NORMS - 1, b * NORMS + 2 * NORMS, b * NORMS + (2 * NORMS - 2))

        @block.scalar
        def _(act):
            act.sem_inc(s_ev, NORMS)
            act.dma_start(wn[:, 0:1], q_norm.rearrange("(p a) -> p a", a=1)).then_inc(s_w, 16)
            act.dma_start(wn[:, 1:2], k_norm.rearrange("(p a) -> p a", a=1)).then_inc(s_w, 16)
            for i, item in enumerate(head_items[:SHARED]):
                hi, lo = split_target(*item)
                act.wait_ge(s_stage[i % 2], 16 * (i // 2 + 1))
                nc.scalar.activation(hi, stage[:, i % 2, :].rearrange("p (j n) -> p j n", j=hi.shape[1]), ACT.Copy)\
                    .then_inc(s_hi, 1)
            act.wait_ge(s_w, 32)
            act.mul(wqs[:, :], wn[:, 0:1], float(DH) ** -0.5).then_inc(s_wqs, 1)
            act.wait_ge(s_wqs, 1)

            def square(u, m, ready):
                act.wait_ge(s_unit, ready)
                nc.scalar.activation(sq[:, m % 2, :], ps_u[:, u % 4, :], ACT.Square).then_inc(s_sq, 1)

            def root(m, ready):
                act.wait_ge(s_var, ready)
                nc.scalar.activation(ss[:, m % 2, 1, :], ss[:, m % 2, 0, :], ACT.Sqrt).then_inc(s_sqrt, 1)

            def copy_out(m, ready, stored, weight):
                act.wait_ge(s_tr, ready)
                act.wait_ge(s_st[m % 2], stored)
                nc.scalar.activation(ev[:, m % 2, :], ps_t[:, m % 2, :], ACT.Copy, scale=weight).then_inc(s_ev, 1)

            def store(m, ready, dst):
                act.wait_ge(s_ev, ready)
                act.dma_start(dst, ev[:, m % 2, :].rearrange("d (h t) -> d h t", h=HPC)).then_inc(s_st[m % 2], 16)

            with act.Fori(0, NB) as b:
                for u, (kind, ci, t) in enumerate(PLAN):
                    if kind == "k":
                        square(u, u, b * UNITS + UNITS + u + 1)
                    if 1 <= u <= K_UNITS:
                        m = u - 1
                        copy_out(m, b * NORMS + NORMS + m + 1, b * (8 * NORMS) + 16 * (m // 2 + 1), wn[:, 1:2])
                        c, tt = m // KT, m % KT
                        store(m, b * NORMS + NORMS + m + 1,
                              k_s[c * HPC:(c + 1) * HPC, bass.ds(b, 1), :, tt * P:(tt + 1) * P]
                              .rearrange("h o d t -> d (h o) t"))
                    if kind == "k":
                        root(u, b * NORMS + u + 1)
                    else:
                        v = u - K_UNITS
                        act.wait_ge(s_unit, b * UNITS + UNITS + u + 1)
                        act.wait_ge(s_vst[v % 2], b * (8 * VUNITS) + 16 * (v // 2 + 1))
                        nc.scalar.activation(vev[:, v % 2, :], ps_u[:, u % 4, :], ACT.Copy).then_inc(s_vev, 1)
                        act.wait_ge(s_vev, b * VUNITS + v + 1)
                        act.dma_start(v_s[(ci - NKV) * HPC:(ci - NKV + 1) * HPC, bass.ds(b, 1), :, t, :]
                                      .rearrange("h o p d -> p (h o) d"),
                                      vev[:, v % 2, :].rearrange("p (h d) -> p h d", h=HPC)).then_inc(s_vst[v % 2], 16)
                    if u < QT:
                        act.wait_ge(s_lnv, b * QT + u + 1)
                        nc.scalar.activation(ln_r[:, u % 2, 0:1], ln_mv[:, u % 2, 1:2], ACT.Sqrt).then_inc(s_lnq, 1)
                    if 2 <= u < 2 + QT:
                        tt = u - 2
                        for e in range(2):
                            act.wait_ge(s_xtr, b * 2 * QT + 2 * QT + 2 * tt + e + 1)
                            nc.scalar.activation(
                                kv_hi[:, e * HPC:(e + 1) * HPC, SC + tt * P:SC + (tt + 1) * P],
                                ps_x[:, e, :].rearrange("p (j t) -> p j t", j=HPC), ACT.Copy).then_inc(s_xhi, 1)

                def q_pass(j):
                    def out_block(r):
                        m = K_UNITS + r
                        copy_out(m, b * NORMS + j * (2 * QT) + (NORMS + m + 1),
                                 b * (8 * NORMS) + j * (16 * QT) + 16 * (m // 2 + 1), wqs[:, 0:1])
                        store(m, b * NORMS + j * (2 * QT) + (NORMS + m + 1),
                              q_s[bass.ds(j * (2 * HPC) + (r // QT) * HPC, HPC), bass.ds(b, 1), :,
                                  (r % QT) * P:(r % QT + 1) * P].rearrange("h o d t -> d (h o) t"))
                    for r in range(2 * QT):
                        m = K_UNITS + r
                        square(r, m, b * UNITS + j * (2 * QT) + (UNITS + 2 * K_UNITS + r + 1))
                        if r >= 1 or not isinstance(j, int):
                            out_block(r - 1)
                        root(m, b * NORMS + j * (2 * QT) + (m + 1))

                q_pass(0)
                with act.Fori(1, NQC // 2) as j:
                    q_pass(j)
                copy_out(NORMS - 1, b * NORMS + 2 * NORMS, b * (8 * NORMS) + 8 * NORMS, wqs[:, 0:1])
                store(NORMS - 1, b * NORMS + 2 * NORMS,
                      q_s[HEADS - HPC:HEADS, bass.ds(b, 1), :, SQ - P:SQ].rearrange("h o d t -> d (h o) t"))
            for s in range(2):
                act.wait_ge(s_st[s], 8 * NB * NORMS + 16)
                act.wait_ge(s_vst[s], 8 * NB * VUNITS + 16)

        @block.vector
        def _(dve):
            dve.sem_inc(s_kn, NORMS)
            dve.sem_inc(s_xlo, 2 * QT)
            for s in range(2):
                dve.sem_inc(s_st[s], 16)
                dve.sem_inc(s_vst[s], 16)
            for i, item in enumerate(head_items[:SHARED]):
                hi, lo = split_target(*item)
                dve.wait_ge(s_hi, i + 1)
                nc.vector.tensor_tensor(lo, stage[:, i % 2, :].rearrange("p (j n) -> p j n", j=hi.shape[1]),
                                        hi.bitcast(F32), ALU.subtract).then_inc(s_lo, 1)

            def norm(u, m, sq_ready, dv, root_ready, tr_free):
                dve.wait_ge(s_sq, sq_ready)
                nc.vector.tensor_reduce(ss[:, m % 2, 2, :], sq[:, m % 2, :].rearrange("p (h d) -> p h d", h=HPC),
                                        AX.X, ALU.add).then_inc(s_dv, 1)
                dve.wait_ge(s_dv, dv)
                nc.vector.tensor_scalar(ss[:, m % 2, 0, :], ss[:, m % 2, 2, :], 1.0 / DH, RMS_EPS, ALU.mult, ALU.add)\
                    .then_inc(s_var, 1)
                dve.wait_ge(s_sqrt, root_ready)
                nc.vector.reciprocal(ss[:, m % 2, 2, :], ss[:, m % 2, 1, :]).then_inc(s_dv, 1)
                dve.wait_ge(s_dv, dv + 1)
                dve.wait_ge(s_tr, tr_free)
                nc.vector.tensor_tensor(kn[:, m % 2, :].rearrange("p (h d) -> p h d", h=HPC),
                                        ps_u[:, u % 4, :].rearrange("p (h d) -> p h d", h=HPC),
                                        ss[:, m % 2, 2, :].rearrange("p (h a) -> p h a", a=1).to_broadcast([P, HPC, DH]),
                                        ALU.mult).then_inc(s_kn, 1)

            DV = 2 * NORMS + 4 * QT
            with dve.Fori(0, NB) as b:
                link = 0
                for u in range(K_UNITS):
                    norm(u, u, b * NORMS + u + 1, b * DV + link + 1, b * NORMS + u + 1, b * NORMS + NORMS + u - 1)
                    link += 2
                    if u < QT:
                        dve.wait_ge(s_x[u % 2], b * (8 * QT) + 16 * (u // 2 + 1))
                        for e in range(2):
                            nc.vector.bn_stats(ln_st[:, u % 2, e, :], xt[:, u % 2, e * 512:(e + 1) * 512]).then_inc(s_dv, 1)
                        link += 2
                        dve.wait_ge(s_dv, b * DV + link)
                        dve.sem_inc(s_carry, 1)
                        nc.vector.bn_aggr(ln_mv[:, u % 2, :], ln_st[:, u % 2, :, :]).then_inc(s_dv, 1)
                        link += 1
                        dve.wait_ge(s_dv, b * DV + link)
                        nc.vector.tensor_scalar(ln_mv[:, u % 2, 1:2], ln_mv[:, u % 2, 1:2], LN_EPS, None, ALU.add).then_inc(s_lnv, 1)
                        dve.wait_ge(s_lnq, b * QT + u + 1)
                        nc.vector.reciprocal(ln_r[:, u % 2, 1:2], ln_r[:, u % 2, 0:1]).then_inc(s_dv, 1)
                        link += 1
                        dve.wait_ge(s_dv, b * DV + link)
                        nc.vector.tensor_scalar(xt[:, u % 2, :], xt[:, u % 2, :], ln_mv[:, u % 2, 0:1], ln_r[:, u % 2, 1:2],
                                                ALU.subtract, ALU.mult).then_inc(s_xn, 1)
                    if 2 <= u < 2 + QT:
                        tt = u - 2
                        for e in range(2):
                            dve.wait_ge(s_xhi, b * 2 * QT + 2 * tt + e + 1)
                            dst = slice(SC + tt * P, SC + (tt + 1) * P)
                            nc.vector.tensor_tensor(
                                kv_lo[:, e * HPC:(e + 1) * HPC, dst],
                                ps_x[:, e, :].rearrange("p (j t) -> p j t", j=HPC),
                                kv_hi[:, e * HPC:(e + 1) * HPC, dst].bitcast(F32), ALU.subtract).then_inc(s_xlo, 1)
                with dve.Fori(0, NQC // 2) as j:
                    for r in range(2 * QT):
                        m = K_UNITS + r
                        norm(r, m, b * NORMS + j * (2 * QT) + (m + 1), b * DV + j * (4 * QT) + (link + 2 * r + 1),
                             b * NORMS + j * (2 * QT) + (m + 1), b * NORMS + j * (2 * QT) + (NORMS + m - 1))


def attention(nc, k_s, v_s, q_s, wo, x, acc, ident):
    BLK = QT * (SK // CW)
    NBLK = SK // CW
    BODY = NB * GRP * BLK
    HB = NB * GRP
    TILES = HB * QT
    LAG_E, LAG_T, LAG_V = 3, BLK + 1, BLK + 3
    LAG_RB = BLK + 5
    LAG_O = LAG_V + BLK - 1
    RB = 4
    N_WO = QT * (D // CW)

    with ExitStack() as ctx:
        def sb(name, shape, dt=F32):
            return ctx.enter_context(nc.sbuf_tensor(name, shape, dt))

        def sem(name):
            return ctx.enter_context(nc.semaphore(name))

        k_hi = sb("k_hi", [P, NB, SK], F32R)
        k_lo = sb("k_lo", [P, NB, SK], F32R)
        v_hi = sb("v_hi", [P, NB, KT, DH], F32R)
        v_lo = sb("v_lo", [P, NB, KT, DH], F32R)
        q_hi = sb("q_hi", [P, 2, SQ], F32R)
        q_lo = sb("q_lo", [P, 2, SQ], F32R)
        wo_hi = sb("wo_hi", [P, GRP, D], F32R)
        wo_lo = sb("wo_lo", [P, GRP, D], F32R)
        stage = sb("stage_b", [P, 2, SK])
        pr = sb("pr", [P, 2, QT, SK])
        pt_hi = sb("pt_hi", [P, 2, SQ], F32R)
        pt_lo = sb("pt_lo", [P, 2, SQ], F32R)
        o_hi = sb("o_hi", [P, GRP, SQ], F32R)
        o_lo = sb("o_lo", [P, GRP, SQ], F32R)
        on = sb("on", [P, SQ])
        mx = sb("mx", [P, 2, QT, NBLK])
        nm = sb("nm", [P, 2, QT])
        rs = sb("rs", [P, 2, QT, NBLK])
        rt = sb("rt", [P, 2, QT])
        ri = sb("ri", [P, 2, QT])
        ps_s = ctx.enter_context(nc.psum_tensor("ps_s", [P, RB, CW], F32))
        ps_p = ctx.enter_context(nc.psum_tensor("ps_p", [P, 2, CW], F32))
        ps_o = ctx.enter_context(nc.psum_tensor("ps_o", [P, SQ], F32))
        ps_m = ctx.enter_context(nc.psum_tensor("ps_m", [P, CW], F32))

        s_stage = [sem("b_stage0"), sem("b_stage1")]
        s_acc = sem("b_acc")
        s_carry = sem("b_carry")
        s_hi = sem("b_hi")
        s_lo = sem("b_lo")
        s_score = sem("b_score")
        s_max = sem("b_max")
        s_nm = sem("b_nm")
        s_exp = sem("b_exp")
        s_rt = sem("b_rt")
        s_ri = sem("b_ri")
        s_rb = sem("b_rb")
        s_on = sem("b_on")
        s_tr = sem("b_tr")
        s_phi = sem("b_phi")
        s_plo = sem("b_plo")
        s_pv = sem("b_pv")
        s_o = sem("b_o")
        s_ohi = sem("b_ohi")
        s_olo = sem("b_olo")
        s_wo = sem("b_wo")
        s_add = sem("b_add")
        block = ctx.enter_context(nc.Block())

        ITEMS = [("k", 0), ("q", 0), ("q", 1), ("v", 0), ("k", 1), ("q", 2), ("v", 1), ("q", 3),
                 ("w", 0), ("w", 1), ("w", 2), ("w", 3), ("q", 4), ("q", 5), ("q", 6), ("q", 7)]
        NI = len(ITEMS)
        DONE = {it: i + 1 for i, it in enumerate(ITEMS)}
        assert NI % 2 == 0
        WO_SLOTS = {LAG_V + GRP * BLK + 4 + u + d: (b, u)
                    for b, d in ((0, 0), (1, GRP * BLK - BODY)) for u in range(N_WO)}
        WO_FIRST = [s for s, (b, u) in WO_SLOTS.items() if u == 0]
        WO_ALL = NB * N_WO
        SHARED = 3

        def split_operands(i):
            kind, n = ITEMS[i]
            if kind == "k":
                return k_hi[:, n, :], k_lo[:, n, :], stage[:, i % 2, :]
            if kind == "v":
                return (v_hi[:, n, :, :].rearrange("p t d -> p (t d)"), v_lo[:, n, :, :].rearrange("p t d -> p (t d)"),
                        stage[:, i % 2, :])
            if kind == "q":
                return q_hi[:, n % 2, :], q_lo[:, n % 2, :], stage[:, i % 2, 0:SQ]
            return wo_hi[:, n, :], wo_lo[:, n, :], stage[:, i % 2, 0:D]

        @block.sync
        def _(sp):
            with sp.Fori(0, KVH) as g:
                for i, (kind, n) in enumerate(ITEMS):
                    sp.wait_ge(s_lo, g * NI + (NI + i - 1))
                    if kind == "k":
                        dst, src = stage[:, i % 2, :], k_s[bass.ds(g, 1), n, :, :].rearrange("o d t -> d (o t)")
                    elif kind == "v":
                        dst = stage[:, i % 2, :]
                        src = v_s[bass.ds(g, 1), n, :, :, :].rearrange("o p t d -> p (o t d)")
                    elif kind == "q":
                        dst = stage[:, i % 2, 0:SQ]
                        src = q_s[bass.ds(g * GRP + n % GRP, 1), n // GRP, :, :].rearrange("o d t -> d (o t)")
                    else:
                        dst, src = stage[:, i % 2, 0:D], wo[bass.ds(g * (GRP * DH) + n * DH, DH), :]
                    sp.dma_start(dst, src).then_inc(s_stage[i % 2], 16)

        @block.gpsimd
        def _(pool):
            pool.sem_inc(s_lo, NI)

            def run(g):
                for i, (kind, n) in enumerate(ITEMS):
                    if isinstance(g, int) and i < SHARED:
                        continue
                    pool.wait_ge(s_stage[i % 2], g * (8 * NI) + 16 * (i // 2 + 1))
                    if kind == "k":
                        pool.wait_ge(s_score, g * BODY + (n + 1) * GRP * BLK)
                    elif kind == "v":
                        pool.wait_ge(s_pv, g * BODY + (n + 1) * GRP * BLK)
                    elif kind == "q":
                        pool.wait_ge(s_score, g * BODY + (BODY + (n - 1) * BLK))
                    else:
                        pool.wait_ge(s_wo, g * (NB * N_WO) + NB * N_WO)
                    hi, lo, raw = split_operands(i)
                    pool.sem_inc(s_carry, 1)
                    nc.gpsimd.tensor_scalar(hi, raw, 1.0, 1.0, ALU.mult, ALU.mult).then_inc(s_hi, 1)
                    pool.wait_ge(s_hi, g * NI + i + 1)
                    nc.gpsimd.tensor_tensor(lo, raw, hi.bitcast(F32), ALU.subtract).then_inc(s_lo, 1)

            pool.wait_ge(s_lo, NI + SHARED)
            run(0)
            with pool.Fori(1, KVH) as g:
                run(g)

        def exists(k, s):
            return not (isinstance(k, int) and (k == 0 and s < 0 or k == KVH and s >= 0))

        def wo_exists(k, s):
            return not (isinstance(k, int) and (k == 0 and WO_SLOTS[s][0] == 1 or k == KVH and WO_SLOTS[s][0] == 0))

        def slots(k):
            return range(BODY if not (isinstance(k, int) and k == KVH) else 2 * BLK + 8)

        @block.tensor
        def _(pe):
            pe.sem_inc(s_score, BODY)
            pe.sem_inc(s_pv, BODY)
            pe.sem_inc(s_wo, NB * N_WO)
            pe.sem_inc(s_tr, BODY)

            def run(k):
                for s in slots(k):
                    if exists(k, s):
                        n, i, c = s // BLK, (s % BLK) // NBLK, s % NBLK
                        if s % (GRP * BLK) == 0:
                            pe.wait_ge(s_lo, k * NI + (NI + DONE["k", n // GRP]))
                        if s % BLK == 0:
                            pe.wait_ge(s_lo, k * NI + (NI + DONE["q", n]))
                        pe.wait_ge(s_exp, k * BODY + (BODY + s - RB + 1))
                        qs, ks, b = slice(i * P, (i + 1) * P), slice(c * CW, (c + 1) * CW), n // GRP
                        split_matmul(nc, ps_s[:, s % RB, :], q_hi[:, n % 2, qs], q_lo[:, n % 2, qs],
                                     k_hi[:, b, ks], k_lo[:, b, ks], True, True).then_inc(s_score, 1)
                    y = s - LAG_V
                    if exists(k, y):
                        n, j = y // BLK % HB, y % BLK
                        if y % (GRP * BLK) == 0:
                            pe.wait_ge(s_lo, k * NI + (NI + DONE["v", n // GRP]))
                        if j == 0:
                            pe.wait_ge(s_o, k * HB + (HB + y // BLK))
                        pe.wait_ge(s_plo, k * BODY + (BODY + y + 1))
                        split_matmul(nc, ps_o[:, :], v_hi[:, n // GRP, j, :], v_lo[:, n // GRP, j, :],
                                     pt_hi[:, j % 2, :], pt_lo[:, j % 2, :], j == 0, j == BLK - 1).then_inc(s_pv, 1)
                    y = s - LAG_T
                    if exists(k, y):
                        n, j = y // BLK % HB, y % BLK
                        if j % QT == 0:
                            pe.wait_ge(s_exp, k * BODY + (BODY + y // BLK * BLK + (QT - 1) * NBLK + j // QT + 1))
                        pe.wait_ge(s_plo, k * BODY + (BODY + y - 1))
                        for i in range(QT):
                            last = nc.tensor.transpose(ps_p[:, j % 2, i * P:(i + 1) * P],
                                                       pr[:, n % 2, i, j * P:(j + 1) * P], ident[:, :])
                        last.then_inc(s_tr, 1)
                    y = s - LAG_RB
                    if y % BLK == 0 and exists(k, y):
                        n = y // BLK % HB
                        before = -N_WO if s < WO_FIRST[1] else 0 if s < WO_FIRST[0] else N_WO
                        pe.wait_ge(s_ri, k * HB + (y // BLK + 1))
                        pe.wait_ge(s_on, k * HB + (HB + y // BLK))
                        pe.wait_ge(s_add, k * WO_ALL + (WO_ALL + before))
                        for i in range(QT):
                            last = nc.tensor.transpose(ps_m[:, i * P:(i + 1) * P],
                                                       ri[:, n % 2, i:i + 1].to_broadcast([P, P]), ident[:, :])
                        last.then_inc(s_rb, 1)
                    if s in WO_SLOTS and wo_exists(k, s):
                        b, u = WO_SLOTS[s]
                        before = u - b * N_WO
                        if u == 0:
                            y = (s - LAG_RB) // BLK
                            if not exists(k, y):
                                y = -1
                            pe.wait_ge(s_on, k * HB + (HB + y + 1))
                            pe.wait_ge(s_olo, k * HB + (HB + (GRP if b == 0 else 0)))
                            if b == 0:
                                pe.wait_ge(s_lo, k * NI + (NI + DONE["w", GRP - 1]))
                        else:
                            pe.wait_ge(s_add, k * WO_ALL + (WO_ALL + before))
                        qs, ws = slice(u // 2 * P, (u // 2 + 1) * P), slice(u % 2 * CW, (u % 2 + 1) * CW)
                        for h in range(GRP):
                            last = split_matmul(nc, ps_m[:, :], o_hi[:, h, qs], o_lo[:, h, qs],
                                                wo_hi[:, h, ws], wo_lo[:, h, ws], h == 0, h == GRP - 1)
                        last.then_inc(s_wo, 1)

            run(0)
            with pe.Fori(1, KVH) as k:
                run(k)
            run(KVH)

        @block.scalar
        def _(act):
            act.sem_inc(s_exp, BODY)
            act.sem_inc(s_on, HB)
            for i in range(SHARED):
                hi, lo, raw = split_operands(i)
                act.wait_ge(s_stage[i % 2], 16 * (i // 2 + 1))
                nc.scalar.activation(hi, raw, ACT.Copy).then_inc(s_hi, 1)

            def run(k):
                for s in slots(k):
                    if isinstance(k, int) and k == 0 and s == 2 * BLK:
                        act.dma_start(acc[:, :, :], x.rearrange("(t p) d -> p t d", p=P)).then_inc(s_acc, 16)
                    y = s - LAG_E
                    if exists(k, y):
                        n, i, c = y // BLK % HB, (y % BLK) // NBLK, y % NBLK
                        if y % BLK == 0:
                            pr_free = k * BODY + (BODY + (y // BLK - 1) * BLK)
                            act.wait_ge(s_tr, pr_free)
                        act.wait_ge(s_nm, k * TILES + (y // NBLK + 1))
                        nc.scalar.activation(pr[:, n % 2, i, c * CW:(c + 1) * CW], ps_s[:, y % RB, :], ACT.Exp,
                                             bias=nm[:, n % 2, i:i + 1],
                                             accum_out=rs[:, n % 2, i, c:c + 1]).then_inc(s_exp, 1)
                    y = s - LAG_T
                    if exists(k, y):
                        j = y % BLK
                        act.wait_ge(s_pv, k * BODY + (BODY + y - 1))
                        act.wait_ge(s_tr, k * BODY + (BODY + y + 1))
                        nc.scalar.activation(pt_hi[:, j % 2, :], ps_p[:, j % 2, :], ACT.Copy).then_inc(s_phi, 1)
                    y = s - LAG_O - 1
                    if y % BLK == 0 and exists(k, y):
                        h = y // BLK % GRP
                        if h == 0:
                            act.wait_ge(s_wo, k * WO_ALL + (WO_ALL + y // BLK // GRP * N_WO))
                        act.wait_ge(s_o, k * HB + (HB + y // BLK + 1))
                        nc.scalar.activation(o_hi[:, h, :], on[:, :], ACT.Copy).then_inc(s_ohi, 1)
                    y = s - LAG_RB - 1
                    if y % BLK == 0 and exists(k, y):
                        act.wait_ge(s_olo, k * HB + (HB + y // BLK))
                        act.wait_ge(s_rb, k * HB + (y // BLK + 1))
                        nc.scalar.activation(on[:, :], ps_m[:, :], ACT.Copy).then_inc(s_on, 1)

            run(0)
            with act.Fori(1, KVH) as k:
                run(k)
            run(KVH)

        @block.vector
        def _(dve):
            dve.sem_inc(s_plo, BODY)
            dve.sem_inc(s_o, HB)
            dve.sem_inc(s_olo, HB)
            dve.sem_inc(s_add, WO_ALL)
            for i in range(SHARED):
                hi, lo, raw = split_operands(i)
                dve.wait_ge(s_hi, i + 1)
                nc.vector.tensor_tensor(lo, raw, hi.bitcast(F32), ALU.subtract).then_inc(s_lo, 1)

            def run(k):
                for s in slots(k):
                    if exists(k, s):
                        n, i, c = s // BLK, (s % BLK) // NBLK, s % NBLK
                        dve.wait_ge(s_score, k * BODY + (BODY + s + 1))
                        nc.vector.reduce_max(mx[:, n % 2, i, c:c + 1], ps_s[:, s % RB, :], AX.X).then_inc(s_max, 1)
                        if c == NBLK - 1:
                            dve.wait_ge(s_max, k * BODY + s + 1)
                            nc.vector.tensor_reduce(nm[:, n % 2, i:i + 1], mx[:, n % 2, i, :], AX.X, ALU.max,
                                                    negate=True).then_inc(s_nm, 1)
                    y = s - LAG_O
                    if y % BLK == 0 and exists(k, y):
                        dve.wait_ge(s_pv, k * BODY + (BODY + y + BLK))
                        dve.wait_ge(s_on, k * HB + (HB + y // BLK + 1))
                        nc.vector.tensor_tensor(on[:, :], ps_o[:, :], on[:, :], ALU.mult).then_inc(s_o, 1)
                    y = s - LAG_T
                    if exists(k, y):
                        j = y % BLK
                        dve.wait_ge(s_phi, k * BODY + (y + 1))
                        nc.vector.tensor_tensor(pt_lo[:, j % 2, :], ps_p[:, j % 2, :], pt_hi[:, j % 2, :].bitcast(F32),
                                                ALU.subtract).then_inc(s_plo, 1)
                    y = s - LAG_RB + 2
                    if y % BLK == 0 and exists(k, y):
                        n = y // BLK % HB
                        dve.wait_ge(s_exp, k * BODY + (BODY + y + BLK))
                        nc.vector.tensor_reduce(rt[:, n % 2, :], rs[:, n % 2, :, :], AX.X, ALU.add).then_inc(s_rt, 1)
                    y = s - LAG_RB + 1
                    if y % BLK == 0 and exists(k, y):
                        n = y // BLK % HB
                        dve.wait_ge(s_rt, k * HB + (y // BLK + 1))
                        nc.vector.reciprocal(ri[:, n % 2, :], rt[:, n % 2, :]).then_inc(s_ri, 1)
                    y = s - LAG_O - 2
                    if y % BLK == 0 and exists(k, y):
                        h = y // BLK % GRP
                        dve.wait_ge(s_ohi, k * HB + (y // BLK + 1))
                        nc.vector.tensor_tensor(o_lo[:, h, :], on[:, :], o_hi[:, h, :].bitcast(F32),
                                                ALU.subtract).then_inc(s_olo, 1)
                    if s in WO_SLOTS and wo_exists(k, s):
                        b, u = WO_SLOTS[s]
                        if isinstance(k, int) and k == 0 and u == 0:
                            dve.wait_ge(s_acc, 16)
                        dve.wait_ge(s_wo, k * WO_ALL + (WO_ALL + u - b * N_WO + 1))
                        part = acc[:, b * QT + u // 2, u % 2 * CW:(u % 2 + 1) * CW]
                        nc.vector.tensor_tensor(part, part, ps_m[:, :], ALU.add).then_inc(s_add, 1)

            run(0)
            with dve.Fori(1, KVH) as k:
                run(k)
            run(KVH)


def experts(nc, a_t, b_r, wr_t, acc, ident, out):
    TOP = 8
    TAKEN = -3.0e38
    MC = KR // P
    RC = P // EXPERTS
    NE = D // CW
    NV = QT * NE

    with ExitStack() as ctx:
        def sb(name, shape, dt=F32):
            return ctx.enter_context(nc.sbuf_tensor(name, shape, dt))

        def sem(name):
            return ctx.enter_context(nc.semaphore(name))

        y_hi = sb("y_hi", [P, DC, SQ], F32R)
        y_lo = sb("y_lo", [P, DC, SQ], F32R)
        h_hi = sb("h_hi", [P, MC, SQ], F32R)
        h_lo = sb("h_lo", [P, MC, SQ], F32R)
        b_hi = sb("b_hi", [P, MC, D], F32R)
        b_lo = sb("b_lo", [P, MC, D], F32R)
        a_hi = sb("a_hi", [P, 2, DC, P], F32R)
        a_lo = sb("a_lo", [P, 2, DC, P], F32R)
        wr_hi = sb("wr_hi", [P, DC, EXPERTS], F32R)
        wr_lo = sb("wr_lo", [P, DC, EXPERTS], F32R)
        stage = sb("stage_c", [P, 2, D])
        yn = sb("yn", [P, 2, D])
        gx = sb("gx", [P, SQ])
        hg = sb("hg", [P, 2, SQ])
        gates = sb("gates", [P, QT, P])
        ln_st = sb("ln_st_c", [P, NE, 6])
        ln_mv = sb("ln_mv_c", [P, 2])
        ln_r = sb("ln_r_c", [P, 2])
        sc = sb("sc", [P, EXPERTS])
        sc2 = sb("sc2", [P, EXPERTS])
        z = sb("z", [P, 2, EXPERTS])
        best = sb("best", [P, 2, TOP])
        row = sb("row", [P, 3])
        ps_x = ctx.enter_context(nc.psum_tensor("ps_xc", [P, NE, CW], F32))
        ps_h = ctx.enter_context(nc.psum_tensor("ps_h", [P, 2, SQ], F32))
        ps_y = ctx.enter_context(nc.psum_tensor("ps_y", [P, 2, CW], F32))
        ps_g = ctx.enter_context(nc.psum_tensor("ps_g", [P, SQ], F32))
        ps_r = ctx.enter_context(nc.psum_tensor("ps_r", [P, EXPERTS], F32))

        s_stage = [sem("c_stage0"), sem("c_stage1")]
        s_hi = sem("c_hi")
        s_bhi = sem("c_bhi")
        s_lo = sem("c_lo")
        s_dv = sem("c_dv")
        s_var = sem("c_var")
        s_root = sem("c_root")
        s_yn = sem("c_yn")
        s_xtr = sem("c_xtr")
        s_xhi = sem("c_xhi")
        s_xlo = sem("c_xlo")
        s_r = sem("c_r")
        s_sc = sem("c_sc")
        s_rmax = sem("c_rmax")
        s_e = sem("c_e")
        s_gate = sem("c_gate")
        s_h = sem("c_h")
        s_g = sem("c_g")
        s_gx = sem("c_gx")
        s_hg = sem("c_hg")
        s_hhi = sem("c_hhi")
        s_hlo = sem("c_hlo")
        s_y = sem("c_y")
        s_ot = sem("c_ot")
        s_out = sem("c_out")
        block = ctx.enter_context(nc.Block())

        ITEMS = [("r", 0, 0), ("a", 0, 0)]
        for m in range(MC):
            if m + 1 < MC:
                ITEMS.append(("a", 0, m + 1))
            ITEMS.append(("b", 0, m))
        ITEMS += [("a", 1, m) for m in range(MC)]
        AT = {it: i for i, it in enumerate(ITEMS)}

        def landed(eng, i):
            eng.wait_ge(s_stage[i % 2], 16 * (i // 2 + 1))

        LN_STEPS = ["n0", "n1", "t0", "n2", "t1", "n3", "t2", "t3", "r0", "r1", "r2", "r3"]
        STEPS = [(s[0], 0, int(s[1])) for s in LN_STEPS]
        STEPS += [("h", 0, m) for m in range(MC + 1)]
        between = [["n0"], ["n1", "t0"], ["n2", "t1"], ["n3", "t2"], ["t3", "r0"], ["r1"], ["r2"], ["r3"]]
        for v in range(NV):
            STEPS += [("y", 0, v)] + [(s[0], 1, int(s[1])) for s in between[v]]
        STEPS += [("h", 1, m) for m in range(MC + 1)] + [("y", 1, v) for v in range(NV)]

        @block.sync
        def _(sp):
            a_view = a_t.rearrange("(j p) n -> p j n", p=P)
            for i, (kind, b, m) in enumerate(ITEMS):
                if i >= 2:
                    sp.wait_ge(s_lo, i - 1)
                if kind == "r":
                    dst = stage[:, i % 2, 0:DC * EXPERTS].rearrange("p (j n) -> p j n", j=DC)
                    src = wr_t.rearrange("(j p) n -> p j n", p=P)
                elif kind == "a":
                    dst = stage[:, i % 2, :].rearrange("p (j n) -> p j n", j=DC)
                    src = a_view[:, :, m * P:(m + 1) * P]
                else:
                    dst, src = stage[:, i % 2, :], b_r[m * P:(m + 1) * P, :]
                sp.dma_start(dst, src).then_inc(s_stage[i % 2], 16)

        @block.gpsimd
        def _(pool):
            n_hi = 0
            for i, (kind, b, m) in enumerate(ITEMS):
                raw = stage[:, i % 2, :]
                if kind == "b":
                    pool.wait_ge(s_bhi, m + 1)
                    nc.gpsimd.tensor_tensor(b_lo[:, m, :], raw, b_hi[:, m, :].bitcast(F32), ALU.subtract)\
                        .then_inc(s_lo, 1)
                    continue
                landed(pool, i)
                if kind == "r":
                    hi, lo, raw = wr_hi[:, :, :], wr_lo[:, :, :], stage[:, i % 2, 0:DC * EXPERTS]
                else:
                    hi, lo = a_hi[:, m % 2, :, :], a_lo[:, m % 2, :, :]
                    if b * MC + m >= 2:
                        pool.wait_ge(s_h, b * MC + m - 1)
                hi, lo = hi.rearrange("p j n -> p (j n)"), lo.rearrange("p j n -> p (j n)")
                nc.gpsimd.tensor_scalar(hi, raw, 1.0, 1.0, ALU.mult, ALU.mult).then_inc(s_hi, 1)
                n_hi += 1
                pool.wait_ge(s_hi, n_hi)
                nc.gpsimd.tensor_tensor(lo, raw, hi.bitcast(F32), ALU.subtract).then_inc(s_lo, 1)

        @block.tensor
        def _(pe):
            for kind, b, n in STEPS:
                if kind == "t":
                    t = b * QT + n
                    pe.wait_ge(s_yn, t + 1)
                    for e in range(NE):
                        if t:
                            pe.wait_ge(s_xlo, NE * (t - 1) + e + 1)
                        for j in range(HPC):
                            c = e * HPC + j
                            last = nc.tensor.transpose(ps_x[:, e, j * P:(j + 1) * P],
                                                       yn[:, t % 2, c * P:(c + 1) * P], ident[:, :])
                        last.then_inc(s_xtr, 1)
                elif kind == "r":
                    t = b * QT + n
                    if t == 0:
                        pe.wait_ge(s_lo, AT["r", 0, 0] + 1)
                    else:
                        pe.wait_ge(s_sc, t)
                    pe.wait_ge(s_xlo, NE * (t + 1))
                    cols = slice(n * P, (n + 1) * P)
                    for j in range(DC):
                        last = split_matmul(nc, ps_r[:, :], y_hi[:, j, cols], y_lo[:, j, cols],
                                            wr_hi[:, j, :], wr_lo[:, j, :], j == 0, j == DC - 1)
                    last.then_inc(s_r, 1)
                elif kind == "h":
                    if n < MC:
                        q = b * MC + n
                        pe.wait_ge(s_lo, AT["a", b, n] + 1)
                        if q >= 2:
                            pe.wait_ge(s_hg, q - 1)
                        for j in range(DC):
                            last = split_matmul(nc, ps_h[:, n % 2, :], a_hi[:, n % 2, j, :], a_lo[:, n % 2, j, :],
                                                y_hi[:, j, :], y_lo[:, j, :], j == 0, j == DC - 1)
                        last.then_inc(s_h, 1)
                    if n == 0:
                        pe.wait_ge(s_gate, RC * QT * (b + 1))
                        if b:
                            pe.wait_ge(s_gx, b)
                        for i in range(QT):
                            last = nc.tensor.transpose(ps_g[:, i * P:(i + 1) * P], gates[:, i, :], ident[:, :])
                        last.then_inc(s_g, 1)
                elif kind == "y":
                    q = b * NV + n
                    i, e = n // NE, n % NE
                    if n == 0:
                        pe.wait_ge(s_hlo, MC * (b + 1))
                        if b == 0:
                            pe.wait_ge(s_lo, AT["b", 0, MC - 1] + 1)
                    if q >= 2:
                        pe.wait_ge(s_ot, q - 1)
                    rows, cols = slice(i * P, (i + 1) * P), slice(e * CW, (e + 1) * CW)
                    for m in range(MC):
                        last = split_matmul(nc, ps_y[:, n % 2, :], h_hi[:, m, rows], h_lo[:, m, rows],
                                            b_hi[:, m, cols], b_lo[:, m, cols], m == 0, m == MC - 1)
                    last.then_inc(s_y, 1)

        @block.scalar
        def _(act):
            for kind, b, n in STEPS:
                t = b * QT + n
                if kind == "n":
                    act.wait_ge(s_var, t + 1)
                    nc.scalar.activation(ln_r[:, 0:1], ln_mv[:, 1:2], ACT.Sqrt).then_inc(s_root, 1)
                elif kind == "t":
                    if b == 1 and n == 0:
                        act.wait_ge(s_h, MC)
                    for e in range(NE):
                        act.wait_ge(s_xtr, NE * t + e + 1)
                        nc.scalar.activation(y_hi[:, e * HPC:(e + 1) * HPC, n * P:(n + 1) * P],
                                             ps_x[:, e, :].rearrange("p (j t) -> p j t", j=HPC), ACT.Copy)\
                            .then_inc(s_xhi, 1)
                elif kind == "r":
                    act.wait_ge(s_rmax, t + 1)
                    nc.scalar.activation(z[:, 1, :], sc[:, :], ACT.Exp, bias=row[:, 0:1]).then_inc(s_e, 1)
                elif kind == "h":
                    if n > 0:
                        m = n - 1
                        q = b * MC + m
                        if m == 0:
                            act.wait_ge(s_g, b + 1)
                            if b:
                                act.wait_ge(s_hg, MC)
                            nc.scalar.activation(gx[:, :], ps_g[:, :], ACT.Copy).then_inc(s_gx, 1)
                        if b == 1 and m == 0:
                            act.wait_ge(s_y, NV)
                        act.wait_ge(s_hg, q + 1)
                        nc.scalar.activation(h_hi[:, m, :], hg[:, m % 2, :], ACT.Copy).then_inc(s_hhi, 1)
                        if b == 0:
                            landed(act, AT["b", 0, m])
                            nc.scalar.activation(b_hi[:, m, :], stage[:, AT["b", 0, m] % 2, :], ACT.Copy)\
                                .then_inc(s_bhi, 1)
                elif kind == "y":
                    q = b * NV + n
                    act.wait_ge(s_ot, q + 1)
                    act.dma_start(out[(b * QT + n // NE) * P:(b * QT + n // NE + 1) * P,
                                      n % NE * CW:(n % NE + 1) * CW],
                                  acc[:, b * QT + n // NE, n % NE * CW:(n % NE + 1) * CW]).then_inc(s_out, 16)
            act.wait_ge(s_out, 16 * NB * NV)

        @block.vector
        def _(dve):
            links = [0]

            def link(ins):
                links[0] += 1
                ins.then_inc(s_dv, 1)
                dve.wait_ge(s_dv, links[0])

            for kind, b, n in STEPS:
                t = b * QT + n
                if kind == "n":
                    for e in range(NE):
                        ins = nc.vector.bn_stats(ln_st[:, e, :], acc[:, t, e * CW:(e + 1) * CW])
                        if e == NE - 1:
                            link(ins)
                    link(nc.vector.bn_aggr(ln_mv[:, :], ln_st[:, :, :]))
                    nc.vector.tensor_scalar(ln_mv[:, 1:2], ln_mv[:, 1:2], LN_EPS, None, ALU.add).then_inc(s_var, 1)
                    dve.wait_ge(s_root, t + 1)
                    link(nc.vector.reciprocal(ln_r[:, 1:2], ln_r[:, 0:1]))
                    if t >= 2:
                        dve.wait_ge(s_xtr, NE * (t - 1))
                    nc.vector.tensor_scalar(yn[:, t % 2, :], acc[:, t, :], ln_mv[:, 0:1], ln_r[:, 1:2],
                                            ALU.subtract, ALU.mult).then_inc(s_yn, 1)
                    dve.wait_ge(s_yn, t + 1)
                elif kind == "t":
                    for e in range(NE):
                        dve.wait_ge(s_xhi, NE * t + e + 1)
                        rows, cols = slice(e * HPC, (e + 1) * HPC), slice(n * P, (n + 1) * P)
                        nc.vector.tensor_tensor(y_lo[:, rows, cols], ps_x[:, e, :].rearrange("p (j t) -> p j t", j=HPC),
                                                y_hi[:, rows, cols].bitcast(F32), ALU.subtract).then_inc(s_xlo, 1)
                elif kind == "r":
                    dve.wait_ge(s_r, t + 1)
                    nc.vector.tensor_copy(sc[:, :], ps_r[:, :]).then_inc(s_sc, 1)
                    dve.wait_ge(s_sc, t + 1)
                    link(nc.vector.max(best[:, 0, :], sc[:, :]))
                    nc.vector.tensor_scalar(row[:, 0:1], best[:, 0, 0:1], -1.0, None, ALU.mult).then_inc(s_rmax, 1)
                    link(nc.vector.match_replace(z[:, 0, :], best[:, 0, :], sc[:, :], TAKEN))
                    link(nc.vector.max(best[:, 1, :], z[:, 0, :]))
                    link(nc.vector.match_replace(sc2[:, :], best[:, 1, :], z[:, 0, :], TAKEN))
                    link(nc.vector.tensor_scalar(z[:, 0, :], sc2[:, :], TAKEN, None, ALU.is_equal))
                    dve.wait_ge(s_e, t + 1)
                    link(nc.vector.tensor_tensor(z[:, 1, :], z[:, 1, :], z[:, 0, :], ALU.mult))
                    link(nc.vector.reduce_sum(row[:, 1:2], z[:, 1, :], AX.X))
                    link(nc.vector.reciprocal(row[:, 2:3], row[:, 1:2]))
                    if b == 1 and n == 0:
                        dve.wait_ge(s_g, 1)
                    for r in range(RC):
                        nc.vector.tensor_scalar(gates[:, n, r * EXPERTS:(r + 1) * EXPERTS], z[:, 1, :], row[:, 2:3],
                                                GATE_SCALE, ALU.mult, ALU.mult).then_inc(s_gate, 1)
                    dve.wait_ge(s_gate, RC * (t + 1))
                elif kind == "h":
                    if n > 0:
                        m = n - 1
                        q = b * MC + m
                        dve.wait_ge(s_h, q + 1)
                        dve.wait_ge(s_gx, b + 1)
                        if q >= 2:
                            dve.wait_ge(s_hlo, q - 1)
                        nc.vector.tensor_tensor(hg[:, m % 2, :], ps_h[:, m % 2, :], gx[:, :], ALU.mult)\
                            .then_inc(s_hg, 1)
                        dve.wait_ge(s_hhi, q + 1)
                        nc.vector.tensor_tensor(h_lo[:, m, :], hg[:, m % 2, :], h_hi[:, m, :].bitcast(F32),
                                                ALU.subtract).then_inc(s_hlo, 1)
                elif kind == "y":
                    q = b * NV + n
                    dve.wait_ge(s_y, q + 1)
                    part = acc[:, b * QT + n // NE, n % NE * CW:(n % NE + 1) * CW]
                    nc.vector.tensor_tensor(part, part, ps_y[:, n % 2, :], ALU.add).then_inc(s_ot, 1)


def cross_attention_and_experts(nc, x, ctx_t, w_kvq, q_norm, k_norm, wo, a_t, b_r, wr_t, out):
    x_rows = x.rearrange("b s d -> (b s) d")
    out_rows = out.rearrange("b s d -> (b s) d")
    k_s = nc.dram_tensor("k_s", (KVH, NB, P, SK), F32, kind="Internal").ap()
    v_s = nc.dram_tensor("v_s", (KVH, NB, P, KT, DH), F32, kind="Internal").ap()
    q_s = nc.dram_tensor("q_s", (HEADS, NB, P, SQ), F32, kind="Internal").ap()
    with nc.sbuf_tensor("ident", [P, P], F32) as ident:
        projections(nc, x_rows, ctx_t, w_kvq, q_norm, k_norm, ident, k_s, v_s, q_s)
        with nc.sbuf_tensor("acc", [P, NB * QT, D], F32) as acc:
            attention(nc, k_s, v_s, q_s, wo, x_rows, acc, ident)
            experts(nc, a_t, b_r, wr_t, acc, ident, out_rows)


def kernel(**inputs):
    import numpy as np
    import concourse.bacc as bacc
    from concourse.bass_utils import run_bass_kernel_spmd as run

    nc = bacc.Bacc("TRN2", target_bir_lowering=False, num_devices=1)
    g = {k: np.asarray(v) for k, v in inputs.items()}
    arrays = {
        "in_x": np.ascontiguousarray(g["x"]),
        "in_ctx_t": np.ascontiguousarray(g["ctx_4096"].transpose(0, 2, 1)),
        "in_w_kvq": np.concatenate([g["L0_xattn_Wk"], g["L0_xattn_Wv"], g["L0_xattn_Wq"]], axis=1),
        "in_q_norm": g["L0_xattn_q_norm_w"],
        "in_k_norm": g["L0_xattn_k_norm_w"],
        "in_wo": g["L0_xattn_Wo"],
        "in_a_t": np.ascontiguousarray(g["L0_ffn_A"].transpose(2, 1, 0).reshape(D, KR)),
        "in_b_r": np.ascontiguousarray(g["L0_ffn_B"].transpose(2, 0, 1).reshape(KR, D)),
        "in_wr_t": np.ascontiguousarray(g["L0_ffn_Wr"].T),
    }
    ins = [nc.dram_tensor(n, a.shape, F32, kind="ExternalInput").ap() for n, a in arrays.items()]
    out = nc.dram_tensor("out_0", (NB, SQ, D), F32, kind="ExternalOutput").ap()
    cross_attention_and_experts(nc, *ins, out)
    r = run(nc, [arrays], core_ids=[0])
    return r.results[0]["out_0"]
```

```python
import concourse.bass as bass
from concourse import mybir
from contextlib import ExitStack

F32 = mybir.dt.float32
F32R = mybir.dt.float32r
ACT = mybir.ActivationFunctionType
ALU = mybir.AluOpType
AX = mybir.AxisListType

P = 128
NB = 2
SQ = 512
SC = 1024
SK = SC + SQ
D = 1024
DC = D // P
HEADS = 32
KVH = 8
DH = 128
GRP = HEADS // KVH
QT = SQ // P
KT = SK // P
CW = 512
HPC = CW // DH
LN_EPS = 1e-5
RMS_EPS = 1e-6
EXPERTS = 64
RANK = 16
KR = EXPERTS * RANK
GATE_SCALE = 32.0 / RANK


def split_matmul(nc, out, w_hi, w_lo, x_hi, x_lo, start, stop):
    nc.tensor.matmul(out, w_hi, x_hi, start=start, stop=False)
    nc.tensor.matmul(out, w_hi, x_lo, start=False, stop=False)
    return nc.tensor.matmul(out, w_lo, x_hi, start=False, stop=stop)


def projections(nc, x, ctx_t, w_kvq, q_norm, k_norm, ident, pre, s_pre, k_s, v_s, q_s):
    NKV = KVH // HPC
    NQC = HEADS // HPC
    CTX_PIECE = 256
    PIECE = DC * CTX_PIECE
    WROWS = PIECE // CW
    WP = DC // WROWS
    CP = SC // CTX_PIECE
    UNITS = 2 * NKV * KT + NQC * QT
    NORMS = NKV * KT + NQC * QT
    VUNITS = NKV * KT
    ITEMS = CP + WP * (2 * NKV + NQC)
    K_UNITS = NKV * KT
    NORM_AT = {0: 0, 1: 1, 3: 2, 4: 3}
    SPREAD_AT = {2: 0, 3: 1, 5: 2, 6: 3}

    with ExitStack() as ctx:
        def sb(name, shape, dt=F32):
            return ctx.enter_context(nc.sbuf_tensor(name, shape, dt))

        def sem(name):
            return ctx.enter_context(nc.semaphore(name))

        kv_hi = sb("kv_hi", [P, DC, SK], F32R)
        kv_lo = sb("kv_lo", [P, DC, SK], F32R)
        w_hi = sb("w_hi", [P, 2, DC, CW], F32R)
        w_lo = sb("w_lo", [P, 2, DC, CW], F32R)
        stage = sb("stage_a", [P, 2, PIECE])
        xt = pre[:, :, :].rearrange("p s n -> p (s n)")[:, 0:2 * D].rearrange("p (s n) -> p s n", s=2)
        sq = sb("sq", [P, 2, CW])
        kn = sb("kn", [P, 2, CW])
        ev = sb("ev", [P, 2, CW])
        vev = sb("vev", [P, 2, CW])
        ln_st = sb("ln_st_a", [P, 2, 2, 6])
        ln_mv = sb("ln_mv_a", [P, 2, 2])
        ln_r = sb("ln_r_a", [P, 2, 2])
        ss = sb("ss", [P, 2, 3, HPC])
        wn = sb("wn", [P, 2])
        wqs = sb("wqs", [P, 1])
        ps_u = ctx.enter_context(nc.psum_tensor("ps_u", [P, 4, CW], F32))
        ps_t = ctx.enter_context(nc.psum_tensor("ps_t", [P, 2, CW], F32))
        ps_x = ctx.enter_context(nc.psum_tensor("ps_x", [P, 2, CW], F32))

        s_stage = [sem("a_stage0"), sem("a_stage1")]
        s_hi = sem("a_hi")
        s_lo = sem("a_lo")
        s_x = [sem("a_x0"), sem("a_x1")]
        s_w = sem("a_w")
        s_wqs = sem("a_wqs")
        s_carry = sem("a_carry")
        s_id = sem("a_id")
        s_unit = sem("a_unit")
        s_sq = sem("a_sq")
        s_dv = sem("a_dv")
        s_var = sem("a_var")
        s_sqrt = sem("a_sqrt")
        s_kn = sem("a_kn")
        s_tr = sem("a_tr")
        s_ev = sem("a_ev")
        s_vev = sem("a_vev")
        s_st = [sem("a_st0"), sem("a_st1")]
        s_vst = [sem("a_vst0"), sem("a_vst1")]
        s_lnv = sem("a_lnv")
        s_lnq = sem("a_lnq")
        s_xn = sem("a_xn")
        s_xtr = sem("a_xtr")
        s_xhi = sem("a_xhi")
        s_xlo = sem("a_xlo")
        block = ctx.enter_context(nc.Block())

        w_view = w_kvq.rearrange("(j p) n -> p j n", p=P)

        head_items = [("w", 0, 0), ("c", 0, 0), ("w", 0, 1), ("c", 0, 1), ("c", 0, 2), ("c", 0, 3)]
        head_items += [("w", ci, p) for ci in range(1, 2 * NKV) for p in range(WP)]
        W_READY = {0: 3, 1: CP + 2 * WP, 2: CP + 3 * WP, 3: CP + 4 * WP}
        C_READY = [2, 4, 5, 6]
        SHARED = 3

        def split_target(kind, ci, p):
            if kind == "w":
                rows = slice(p * WROWS, (p + 1) * WROWS)
                return w_hi[:, ci % 2, rows, :], w_lo[:, ci % 2, rows, :]
            cols = slice(p * CTX_PIECE, (p + 1) * CTX_PIECE)
            return kv_hi[:, :, cols], kv_lo[:, :, cols]

        @block.sync
        def _(sp):
            def load(item, free, src):
                sp.wait_ge(s_lo, free)
                sp.dma_start(stage[:, item % 2, :].rearrange("p (j n) -> p j n", j=src.shape[1]),
                             src).then_inc(s_stage[item % 2], 16)

            with sp.Fori(0, NB) as b:
                ctx_b = ctx_t[bass.ds(b, 1), :, :].rearrange("o (j p) t -> p (o j) t", p=P)
                for i, (kind, ci, p) in enumerate(head_items):
                    if kind == "w":
                        src = w_view[:, p * WROWS:(p + 1) * WROWS, ci * CW:(ci + 1) * CW]
                    else:
                        src = ctx_b[:, :, p * CTX_PIECE:(p + 1) * CTX_PIECE]
                    load(i, b * ITEMS + ITEMS + i - 1, src)
                    if i == SHARED - 1:
                        for t in range(2):
                            sp.wait_ge(s_xtr, b * 2 * QT + 2 * QT)
                            sp.dma_start(xt[:, t, :], x[bass.ds(b * SQ + t * P, P), :]).then_inc(s_x[t], 16)
                    if i == 5:
                        for t in range(2, QT):
                            sp.wait_ge(s_xtr, b * 2 * QT + 2 * QT + 2 * (t - 1))
                            sp.dma_start(xt[:, t % 2, :], x[bass.ds(b * SQ + t * P, P), :]).then_inc(s_x[t % 2], 16)
                with sp.Fori(0, NQC // 2) as j:
                    for c in range(2):
                        for p in range(WP):
                            i = len(head_items) + c * WP + p
                            load(i, b * ITEMS + j * (2 * WP) + (ITEMS + i - 1),
                                 w_view[:, p * WROWS:(p + 1) * WROWS, bass.ds(j * (2 * CW) + (2 * NKV + c) * CW, CW)])

            for h in range(2):
                sp.wait_ge(s_st[h], 8 * NORMS + 16)
            sp.wait_ge(s_xtr, NB * 2 * QT + 2 * QT)
            sp.dma_start(pre[:, 0, 0:SQ], q_s[0, 0, :, :]).then_inc(s_pre[0], 16)
            sp.dma_start(pre[:, 1, :], k_s[0, 0, :, :]).then_inc(s_pre[1], 16)

        @block.gpsimd
        def _(pool):
            pool.sem_inc(s_lo, ITEMS)
            nc.gpsimd.memset(ident[:, :], 0.0).then_inc(s_id, 1)
            pool.wait_ge(s_id, 1)
            nc.gpsimd.affine_select(out=ident[:, :], in_=ident[:, :], compare_op=ALU.not_equal, fill=1.0, base=0,
                                    pattern=[[-1, P]], channel_multiplier=1).then_inc(s_id, 1)

            def split(item, ready, done, free, hi, lo):
                raw = stage[:, item % 2, :].rearrange("p (j n) -> p j n", j=hi.shape[1])
                pool.wait_ge(s_stage[item % 2], ready)
                pool.wait_ge(s_unit, free)
                pool.sem_inc(s_carry, 1)
                nc.gpsimd.tensor_scalar(hi, raw, 1.0, 1.0, ALU.mult, ALU.mult).then_inc(s_hi, 1)
                pool.wait_ge(s_hi, done)
                nc.gpsimd.tensor_tensor(lo, raw, hi.bitcast(F32), ALU.subtract).then_inc(s_lo, 1)

            def batch(b, first):
                for i, (kind, ci, p) in enumerate(head_items):
                    if first and i < SHARED:
                        continue
                    hi, lo = split_target(kind, ci, p)
                    if kind == "w":
                        free = (-QT, 0, KT, 2 * KT)[ci]
                    else:
                        free = -NQC * QT
                    split(i, b * (8 * ITEMS) + 16 * (i // 2 + 1), b * ITEMS + i + 1,
                          b * UNITS + UNITS + free, hi, lo)
                with pool.Fori(0, NQC // 2) as j:
                    for c in range(2):
                        for p in range(WP):
                            i = len(head_items) + c * WP + p
                            rows = slice(p * WROWS, (p + 1) * WROWS)
                            split(i, b * (8 * ITEMS) + j * (16 * WP) + 16 * (i // 2 + 1),
                                  b * ITEMS + j * (2 * WP) + i + 1,
                                  b * UNITS + j * (2 * QT) + (UNITS + 4 * KT - (QT if c == 0 else 0)),
                                  w_hi[:, c, rows, :], w_lo[:, c, rows, :])

            pool.wait_ge(s_lo, ITEMS + SHARED)
            batch(0, True)
            with pool.Fori(1, NB) as b:
                batch(b, False)

        def unit_plan():
            return ([("k", c, t) for c in range(NKV) for t in range(KT)]
                    + [("v", NKV + c, t) for c in range(NKV) for t in range(KT)])

        PLAN = unit_plan()

        @block.tensor
        def _(pe):
            pe.sem_inc(s_unit, UNITS)
            pe.sem_inc(s_xtr, 2 * QT)
            pe.sem_inc(s_tr, NORMS)
            pe.wait_ge(s_id, 2)

            def product(u, wbuf, t, rest_ready=None):
                cols = slice(t * P, (t + 1) * P)
                for j in range(DC):
                    if rest_ready is not None and j == WROWS:
                        pe.wait_ge(s_lo, rest_ready)
                    last = split_matmul(nc, ps_u[:, u % 4, :], kv_hi[:, j, cols], kv_lo[:, j, cols],
                                        w_hi[:, wbuf, j, :], w_lo[:, wbuf, j, :], j == 0, j == DC - 1)
                last.then_inc(s_unit, 1)

            def transposes(m, ready, free):
                pe.wait_ge(s_kn, ready)
                pe.wait_ge(s_ev, free)
                for h in range(HPC):
                    last = nc.tensor.transpose(ps_t[:, m % 2, h * P:(h + 1) * P], kn[:, m % 2, h * P:(h + 1) * P],
                                               ident[:, :])
                last.then_inc(s_tr, 1)

            with pe.Fori(0, NB) as b:
                for u, (kind, ci, t) in enumerate(PLAN):
                    if t == 0 and u > 0:
                        pe.wait_ge(s_lo, b * ITEMS + ITEMS + W_READY[ci])
                    if u % 2 == 0 and u < 2 * CP:
                        pe.wait_ge(s_lo, b * ITEMS + ITEMS + C_READY[u // 2])
                    if u == 2 * CP:
                        pe.wait_ge(s_xlo, b * 2 * QT + 4 * QT)
                    if u < K_UNITS + 4:
                        pe.wait_ge(s_kn, b * NORMS + NORMS + u - 3)
                    else:
                        pe.wait_ge(s_vev, b * VUNITS + (u - K_UNITS - 3))
                    product(u, ci % 2, t, b * ITEMS + ITEMS + W_READY[0] if u == 0 else None)
                    if u in SPREAD_AT:
                        tt = SPREAD_AT[u]
                        for e in range(2):
                            n = 2 * tt + e
                            pe.wait_ge(s_xn, b * QT + tt + 1)
                            pe.wait_ge(s_xlo, b * 2 * QT + (n + 2 * QT - 1))
                            for j in range(HPC):
                                last = nc.tensor.transpose(
                                    ps_x[:, e, j * P:(j + 1) * P],
                                    xt[:, tt % 2, (e * HPC + j) * P:(e * HPC + j + 1) * P], ident[:, :])
                            last.then_inc(s_xtr, 1)
                    if 1 <= u <= K_UNITS:
                        m = u - 1
                        transposes(m, b * NORMS + NORMS + m + 1, b * NORMS + NORMS + m - 1)

                def q_pass(j):
                    for c in range(2):
                        for t in range(QT):
                            r = c * QT + t
                            if t == 0:
                                pe.wait_ge(s_lo, b * ITEMS + j * (2 * WP) + ITEMS + CP + (2 * NKV + c + 1) * WP)
                            m = K_UNITS + r
                            if r < 4:
                                pe.wait_ge(s_vev, b * VUNITS + VUNITS)
                            pe.wait_ge(s_kn, b * NORMS + j * (2 * QT) + (NORMS + m - 3))
                            product(r, c, (KT - QT) + t)
                            if r >= 1 or not isinstance(j, int):
                                transposes(m - 1, b * NORMS + j * (2 * QT) + (NORMS + m),
                                           b * NORMS + j * (2 * QT) + (NORMS + m - 2))

                q_pass(0)
                with pe.Fori(1, NQC // 2) as j:
                    q_pass(j)
                transposes(NORMS - 1, b * NORMS + 2 * NORMS, b * NORMS + (2 * NORMS - 2))

        @block.scalar
        def _(act):
            act.sem_inc(s_ev, NORMS)
            act.dma_start(wn[:, 0:1], q_norm.rearrange("(p a) -> p a", a=1)).then_inc(s_w, 16)
            act.dma_start(wn[:, 1:2], k_norm.rearrange("(p a) -> p a", a=1)).then_inc(s_w, 16)
            for i, item in enumerate(head_items[:SHARED]):
                hi, lo = split_target(*item)
                act.wait_ge(s_stage[i % 2], 16 * (i // 2 + 1))
                nc.scalar.activation(hi, stage[:, i % 2, :].rearrange("p (j n) -> p j n", j=hi.shape[1]), ACT.Copy)\
                    .then_inc(s_hi, 1)
            act.wait_ge(s_w, 32)
            act.mul(wqs[:, :], wn[:, 0:1], float(DH) ** -0.5).then_inc(s_wqs, 1)
            act.wait_ge(s_wqs, 1)

            def square(u, m, ready):
                act.wait_ge(s_unit, ready)
                nc.scalar.activation(sq[:, m % 2, :], ps_u[:, u % 4, :], ACT.Square).then_inc(s_sq, 1)

            def root(m, ready):
                act.wait_ge(s_var, ready)
                nc.scalar.activation(ss[:, m % 2, 1, :], ss[:, m % 2, 0, :], ACT.Sqrt).then_inc(s_sqrt, 1)

            def copy_out(m, ready, stored, weight):
                act.wait_ge(s_tr, ready)
                act.wait_ge(s_st[m % 2], stored)
                nc.scalar.activation(ev[:, m % 2, :], ps_t[:, m % 2, :], ACT.Copy, scale=weight).then_inc(s_ev, 1)

            def store(m, ready, dst):
                act.wait_ge(s_ev, ready)
                act.dma_start(dst, ev[:, m % 2, :].rearrange("d (h t) -> d h t", h=HPC)).then_inc(s_st[m % 2], 16)

            with act.Fori(0, NB) as b:
                for u, (kind, ci, t) in enumerate(PLAN):
                    if kind == "k":
                        square(u, u, b * UNITS + UNITS + u + 1)
                    if 1 <= u <= K_UNITS:
                        m = u - 1
                        copy_out(m, b * NORMS + NORMS + m + 1, b * (8 * NORMS) + 16 * (m // 2 + 1), wn[:, 1:2])
                        c, tt = m // KT, m % KT
                        store(m, b * NORMS + NORMS + m + 1,
                              k_s[c * HPC:(c + 1) * HPC, bass.ds(b, 1), :, tt * P:(tt + 1) * P]
                              .rearrange("h o d t -> d (h o) t"))
                    if kind == "k":
                        root(u, b * NORMS + u + 1)
                    else:
                        v = u - K_UNITS
                        act.wait_ge(s_unit, b * UNITS + UNITS + u + 1)
                        act.wait_ge(s_vst[v % 2], b * (8 * VUNITS) + 16 * (v // 2 + 1))
                        nc.scalar.activation(vev[:, v % 2, :], ps_u[:, u % 4, :], ACT.Copy).then_inc(s_vev, 1)
                        act.wait_ge(s_vev, b * VUNITS + v + 1)
                        act.dma_start(v_s[(ci - NKV) * HPC:(ci - NKV + 1) * HPC, bass.ds(b, 1), :, t, :]
                                      .rearrange("h o p d -> p (h o) d"),
                                      vev[:, v % 2, :].rearrange("p (h d) -> p h d", h=HPC)).then_inc(s_vst[v % 2], 16)
                    if u in SPREAD_AT:
                        tt = SPREAD_AT[u]
                        for e in range(2):
                            act.wait_ge(s_xtr, b * 2 * QT + 2 * QT + 2 * tt + e + 1)
                            nc.scalar.activation(
                                kv_hi[:, e * HPC:(e + 1) * HPC, SC + tt * P:SC + (tt + 1) * P],
                                ps_x[:, e, :].rearrange("p (j t) -> p j t", j=HPC), ACT.Copy).then_inc(s_xhi, 1)
                    if u in NORM_AT:
                        tt = NORM_AT[u]
                        act.wait_ge(s_lnv, b * QT + tt + 1)
                        nc.scalar.activation(ln_r[:, tt % 2, 0:1], ln_mv[:, tt % 2, 1:2], ACT.Sqrt).then_inc(s_lnq, 1)

                def q_pass(j):
                    def out_block(r):
                        m = K_UNITS + r
                        copy_out(m, b * NORMS + j * (2 * QT) + (NORMS + m + 1),
                                 b * (8 * NORMS) + j * (16 * QT) + 16 * (m // 2 + 1), wqs[:, 0:1])
                        store(m, b * NORMS + j * (2 * QT) + (NORMS + m + 1),
                              q_s[bass.ds(j * (2 * HPC) + (r // QT) * HPC, HPC), bass.ds(b, 1), :,
                                  (r % QT) * P:(r % QT + 1) * P].rearrange("h o d t -> d (h o) t"))
                    for r in range(2 * QT):
                        m = K_UNITS + r
                        square(r, m, b * UNITS + j * (2 * QT) + (UNITS + 2 * K_UNITS + r + 1))
                        if r >= 1 or not isinstance(j, int):
                            out_block(r - 1)
                        root(m, b * NORMS + j * (2 * QT) + (m + 1))

                q_pass(0)
                with act.Fori(1, NQC // 2) as j:
                    q_pass(j)
                copy_out(NORMS - 1, b * NORMS + 2 * NORMS, b * (8 * NORMS) + 8 * NORMS, wqs[:, 0:1])
                store(NORMS - 1, b * NORMS + 2 * NORMS,
                      q_s[HEADS - HPC:HEADS, bass.ds(b, 1), :, SQ - P:SQ].rearrange("h o d t -> d (h o) t"))
            for s in range(2):
                act.wait_ge(s_st[s], 8 * NB * NORMS + 16)
                act.wait_ge(s_vst[s], 8 * NB * VUNITS + 16)

        @block.vector
        def _(dve):
            dve.sem_inc(s_kn, NORMS)
            dve.sem_inc(s_xlo, 2 * QT)
            for s in range(2):
                dve.sem_inc(s_st[s], 16)
                dve.sem_inc(s_vst[s], 16)
            for i, item in enumerate(head_items[:SHARED]):
                hi, lo = split_target(*item)
                dve.wait_ge(s_hi, i + 1)
                nc.vector.tensor_tensor(lo, stage[:, i % 2, :].rearrange("p (j n) -> p j n", j=hi.shape[1]),
                                        hi.bitcast(F32), ALU.subtract).then_inc(s_lo, 1)

            def norm(u, m, sq_ready, dv, root_ready, tr_free):
                dve.wait_ge(s_sq, sq_ready)
                nc.vector.tensor_reduce(ss[:, m % 2, 2, :], sq[:, m % 2, :].rearrange("p (h d) -> p h d", h=HPC),
                                        AX.X, ALU.add).then_inc(s_dv, 1)
                dve.wait_ge(s_dv, dv)
                nc.vector.tensor_scalar(ss[:, m % 2, 0, :], ss[:, m % 2, 2, :], 1.0 / DH, RMS_EPS, ALU.mult, ALU.add)\
                    .then_inc(s_var, 1)
                dve.wait_ge(s_sqrt, root_ready)
                nc.vector.reciprocal(ss[:, m % 2, 2, :], ss[:, m % 2, 1, :]).then_inc(s_dv, 1)
                dve.wait_ge(s_dv, dv + 1)
                dve.wait_ge(s_tr, tr_free)
                nc.vector.tensor_tensor(kn[:, m % 2, :].rearrange("p (h d) -> p h d", h=HPC),
                                        ps_u[:, u % 4, :].rearrange("p (h d) -> p h d", h=HPC),
                                        ss[:, m % 2, 2, :].rearrange("p (h a) -> p h a", a=1).to_broadcast([P, HPC, DH]),
                                        ALU.mult).then_inc(s_kn, 1)

            DV = 2 * NORMS + 4 * QT
            with dve.Fori(0, NB) as b:
                link = 0
                for u in range(K_UNITS):
                    norm(u, u, b * NORMS + u + 1, b * DV + link + 1, b * NORMS + u + 1, b * NORMS + NORMS + u - 1)
                    link += 2
                    if u in SPREAD_AT:
                        tt = SPREAD_AT[u]
                        for e in range(2):
                            dve.wait_ge(s_xhi, b * 2 * QT + 2 * tt + e + 1)
                            dst = slice(SC + tt * P, SC + (tt + 1) * P)
                            nc.vector.tensor_tensor(
                                kv_lo[:, e * HPC:(e + 1) * HPC, dst],
                                ps_x[:, e, :].rearrange("p (j t) -> p j t", j=HPC),
                                kv_hi[:, e * HPC:(e + 1) * HPC, dst].bitcast(F32), ALU.subtract).then_inc(s_xlo, 1)
                    if u in NORM_AT:
                        tt = NORM_AT[u]
                        dve.wait_ge(s_x[tt % 2], b * (8 * QT) + 16 * (tt // 2 + 1))
                        for e in range(2):
                            nc.vector.bn_stats(ln_st[:, tt % 2, e, :], xt[:, tt % 2, e * 512:(e + 1) * 512]).then_inc(s_dv, 1)
                        link += 2
                        dve.wait_ge(s_dv, b * DV + link)
                        dve.sem_inc(s_carry, 1)
                        nc.vector.bn_aggr(ln_mv[:, tt % 2, :], ln_st[:, tt % 2, :, :]).then_inc(s_dv, 1)
                        link += 1
                        dve.wait_ge(s_dv, b * DV + link)
                        nc.vector.tensor_scalar(ln_mv[:, tt % 2, 1:2], ln_mv[:, tt % 2, 1:2], LN_EPS, None, ALU.add).then_inc(s_lnv, 1)
                        dve.wait_ge(s_lnq, b * QT + tt + 1)
                        nc.vector.reciprocal(ln_r[:, tt % 2, 1:2], ln_r[:, tt % 2, 0:1]).then_inc(s_dv, 1)
                        link += 1
                        dve.wait_ge(s_dv, b * DV + link)
                        nc.vector.tensor_scalar(xt[:, tt % 2, :], xt[:, tt % 2, :], ln_mv[:, tt % 2, 0:1], ln_r[:, tt % 2, 1:2],
                                                ALU.subtract, ALU.mult).then_inc(s_xn, 1)
                with dve.Fori(0, NQC // 2) as j:
                    for r in range(2 * QT):
                        m = K_UNITS + r
                        norm(r, m, b * NORMS + j * (2 * QT) + (m + 1), b * DV + j * (4 * QT) + (link + 2 * r + 1),
                             b * NORMS + j * (2 * QT) + (m + 1), b * NORMS + j * (2 * QT) + (NORMS + m - 1))


def attention(nc, k_s, v_s, q_s, wo, x, acc, ident, stage, s_stage):
    BLK = QT * (SK // CW)
    NBLK = SK // CW
    BODY = NB * GRP * BLK
    HB = NB * GRP
    TILES = HB * QT
    LAG_E, LAG_T, LAG_V = 3, BLK + 2, BLK + 4
    LAG_RB = BLK + 6
    LAG_O = LAG_V + BLK - 1
    RB = 4
    N_WO = QT * (D // CW)

    with ExitStack() as ctx:
        def sb(name, shape, dt=F32):
            return ctx.enter_context(nc.sbuf_tensor(name, shape, dt))

        def sem(name):
            return ctx.enter_context(nc.semaphore(name))

        k_hi = sb("k_hi", [P, NB, SK], F32R)
        k_lo = sb("k_lo", [P, NB, SK], F32R)
        v_hi = sb("v_hi", [P, NB, KT, DH], F32R)
        v_lo = sb("v_lo", [P, NB, KT, DH], F32R)
        q_hi = sb("q_hi", [P, 2, SQ], F32R)
        q_lo = sb("q_lo", [P, 2, SQ], F32R)
        wo_hi = sb("wo_hi", [P, GRP, D], F32R)
        wo_lo = sb("wo_lo", [P, GRP, D], F32R)
        pr = sb("pr", [P, 2, QT, SK])
        pt_hi = sb("pt_hi", [P, 2, SQ], F32R)
        pt_lo = sb("pt_lo", [P, 2, SQ], F32R)
        o_hi = sb("o_hi", [P, GRP, SQ], F32R)
        o_lo = sb("o_lo", [P, GRP, SQ], F32R)
        on = sb("on", [P, SQ])
        mx = sb("mx", [P, 2, QT, NBLK])
        nm = sb("nm", [P, 2, QT])
        rs = sb("rs", [P, 2, QT, NBLK])
        rt = sb("rt", [P, 2, QT])
        ri = sb("ri", [P, 2, QT])
        ps_s = ctx.enter_context(nc.psum_tensor("ps_s", [P, RB, CW], F32))
        ps_p = ctx.enter_context(nc.psum_tensor("ps_p", [P, 2, CW], F32))
        ps_o = ctx.enter_context(nc.psum_tensor("ps_o", [P, SQ], F32))
        ps_m = ctx.enter_context(nc.psum_tensor("ps_m", [P, CW], F32))

        s_acc = sem("b_acc")
        s_carry = sem("b_carry")
        s_hi = sem("b_hi")
        s_khi = sem("b_khi")
        s_klo = sem("b_klo")
        s_lo = sem("b_lo")
        s_score = sem("b_score")
        s_max = sem("b_max")
        s_nm = sem("b_nm")
        s_exp = sem("b_exp")
        s_rt = sem("b_rt")
        s_ri = sem("b_ri")
        s_rb = sem("b_rb")
        s_on = sem("b_on")
        s_tr = sem("b_tr")
        s_phi = sem("b_phi")
        s_plo = sem("b_plo")
        s_pv = sem("b_pv")
        s_o = sem("b_o")
        s_ohi = sem("b_ohi")
        s_olo = sem("b_olo")
        s_wo = sem("b_wo")
        s_add = sem("b_add")
        block = ctx.enter_context(nc.Block())

        ITEMS = [("q", 0), ("k", 0), ("q", 1), ("v", 0), ("k", 1), ("q", 2), ("v", 1), ("q", 3),
                 ("w", 0), ("w", 1), ("w", 2), ("w", 3), ("q", 4), ("q", 5), ("q", 6), ("q", 7)]
        NI = len(ITEMS)
        DONE = {it: i + 1 for i, it in enumerate(ITEMS)}
        assert NI % 2 == 0
        WO_SLOTS = {LAG_V + GRP * BLK + 4 + u + d: (b, u)
                    for b, d in ((0, 0), (1, GRP * BLK - BODY)) for u in range(N_WO)}
        WO_FIRST = [s for s, (b, u) in WO_SLOTS.items() if u == 0]
        WO_ALL = NB * N_WO
        LOADED = 2
        SHARED = 3

        def split_operands(i):
            kind, n = ITEMS[i]
            if kind == "k":
                return k_hi[:, n, :], k_lo[:, n, :], stage[:, i % 2, :]
            if kind == "v":
                return (v_hi[:, n, :, :].rearrange("p t d -> p (t d)"), v_lo[:, n, :, :].rearrange("p t d -> p (t d)"),
                        stage[:, i % 2, :])
            if kind == "q":
                return q_hi[:, n % 2, :], q_lo[:, n % 2, :], stage[:, i % 2, 0:SQ]
            return wo_hi[:, n, :], wo_lo[:, n, :], stage[:, i % 2, 0:D]

        @block.sync
        def _(sp):
            def run(g):
                for i, (kind, n) in enumerate(ITEMS):
                    if isinstance(g, int) and i < LOADED:
                        continue
                    sp.wait_ge(s_lo, g * NI + (NI + i - 1))
                    if kind == "k":
                        dst, src = stage[:, i % 2, :], k_s[bass.ds(g, 1), n, :, :].rearrange("o d t -> d (o t)")
                    elif kind == "v":
                        dst = stage[:, i % 2, :]
                        src = v_s[bass.ds(g, 1), n, :, :, :].rearrange("o p t d -> p (o t d)")
                    elif kind == "q":
                        dst = stage[:, i % 2, 0:SQ]
                        src = q_s[bass.ds(g * GRP + n % GRP, 1), n // GRP, :, :].rearrange("o d t -> d (o t)")
                    else:
                        dst, src = stage[:, i % 2, 0:D], wo[bass.ds(g * (GRP * DH) + n * DH, DH), :]
                    sp.dma_start(dst, src).then_inc(s_stage[i % 2], 16)

            run(0)
            with sp.Fori(1, KVH) as g:
                run(g)

        @block.gpsimd
        def _(pool):
            pool.sem_inc(s_lo, NI)

            def run(g):
                for i, (kind, n) in enumerate(ITEMS):
                    if isinstance(g, int) and i < SHARED:
                        continue
                    pool.wait_ge(s_stage[i % 2], g * (8 * NI) + 16 * (i // 2 + 1))
                    if kind == "k":
                        pool.wait_ge(s_score, g * BODY + (n + 1) * GRP * BLK)
                    elif kind == "v":
                        pool.wait_ge(s_pv, g * BODY + (n + 1) * GRP * BLK)
                    elif kind == "q":
                        pool.wait_ge(s_score, g * BODY + (BODY + (n - 1) * BLK))
                    else:
                        pool.wait_ge(s_wo, g * (NB * N_WO) + NB * N_WO)
                    hi, lo, raw = split_operands(i)
                    pool.sem_inc(s_carry, 1)
                    nc.gpsimd.tensor_scalar(hi, raw, 1.0, 1.0, ALU.mult, ALU.mult).then_inc(s_hi, 1)
                    pool.wait_ge(s_hi, g * NI + i + 1)
                    nc.gpsimd.tensor_tensor(lo, raw, hi.bitcast(F32), ALU.subtract).then_inc(s_lo, 1)

            pool.wait_ge(s_lo, NI + SHARED)
            run(0)
            with pool.Fori(1, KVH) as g:
                run(g)

        def exists(k, s):
            return not (isinstance(k, int) and (k == 0 and s < 0 or k == KVH and s >= 0))

        def wo_exists(k, s):
            return not (isinstance(k, int) and (k == 0 and WO_SLOTS[s][0] == 1 or k == KVH and WO_SLOTS[s][0] == 0))

        def last_units(k):
            return isinstance(k, int) and k == KVH

        def wo_bank(k, u):
            return ps_o[:, :] if last_units(k) and u % 2 else ps_m[:, :]

        def slots(k):
            return range(BODY if not (isinstance(k, int) and k == KVH) else 2 * BLK + 8)

        @block.tensor
        def _(pe):
            pe.sem_inc(s_score, BODY)
            pe.sem_inc(s_pv, BODY)
            pe.sem_inc(s_wo, NB * N_WO)
            pe.sem_inc(s_tr, BODY)

            def run(k):
                for s in slots(k):
                    if exists(k, s):
                        n, i, c = s // BLK, (s % BLK) // NBLK, s % NBLK
                        if isinstance(k, int) and k == 0 and s < NBLK:
                            pe.wait_ge(s_klo, s + 1)
                        elif s % (GRP * BLK) == 0:
                            pe.wait_ge(s_lo, k * NI + (NI + DONE["k", n // GRP]))
                        if s % BLK == 0:
                            pe.wait_ge(s_lo, k * NI + (NI + DONE["q", n]))
                        pe.wait_ge(s_exp, k * BODY + (BODY + s - RB + 1))
                        qs, ks, b = slice(i * P, (i + 1) * P), slice(c * CW, (c + 1) * CW), n // GRP
                        split_matmul(nc, ps_s[:, s % RB, :], q_hi[:, n % 2, qs], q_lo[:, n % 2, qs],
                                     k_hi[:, b, ks], k_lo[:, b, ks], True, True).then_inc(s_score, 1)
                    y = s - LAG_V
                    if exists(k, y):
                        n, j = y // BLK % HB, y % BLK
                        if y % (GRP * BLK) == 0:
                            pe.wait_ge(s_lo, k * NI + (NI + DONE["v", n // GRP]))
                        if j == 0:
                            pe.wait_ge(s_o, k * HB + (HB + y // BLK))
                        pe.wait_ge(s_plo, k * BODY + (BODY + y + 1))
                        split_matmul(nc, ps_o[:, :], v_hi[:, n // GRP, j, :], v_lo[:, n // GRP, j, :],
                                     pt_hi[:, j % 2, :], pt_lo[:, j % 2, :], j == 0, j == BLK - 1).then_inc(s_pv, 1)
                    y = s - LAG_T
                    if exists(k, y):
                        n, j = y // BLK % HB, y % BLK
                        if j % QT == 0:
                            pe.wait_ge(s_exp, k * BODY + (BODY + y // BLK * BLK + (QT - 1) * NBLK + j // QT + 1))
                        pe.wait_ge(s_plo, k * BODY + (BODY + y - 1))
                        for i in range(QT):
                            last = nc.tensor.transpose(ps_p[:, j % 2, i * P:(i + 1) * P],
                                                       pr[:, n % 2, i, j * P:(j + 1) * P], ident[:, :])
                        last.then_inc(s_tr, 1)
                    y = s - LAG_RB
                    if y % BLK == 0 and exists(k, y):
                        n = y // BLK % HB
                        before = -N_WO if s < WO_FIRST[1] else 0 if s < WO_FIRST[0] else N_WO
                        pe.wait_ge(s_ri, k * HB + (y // BLK + 1))
                        pe.wait_ge(s_on, k * HB + (HB + y // BLK))
                        pe.wait_ge(s_add, k * WO_ALL + (WO_ALL + before))
                        for i in range(QT):
                            last = nc.tensor.transpose(ps_m[:, i * P:(i + 1) * P],
                                                       ri[:, n % 2, i:i + 1].to_broadcast([P, P]), ident[:, :])
                        last.then_inc(s_rb, 1)
                    if s in WO_SLOTS and wo_exists(k, s):
                        b, u = WO_SLOTS[s]
                        before = u - b * N_WO
                        if u == 0:
                            y = (s - LAG_RB) // BLK
                            if not exists(k, y):
                                y = -1
                            pe.wait_ge(s_on, k * HB + (HB + y + 1))
                            pe.wait_ge(s_olo, k * HB + (HB + (GRP if b == 0 else 0)))
                            if b == 0:
                                pe.wait_ge(s_lo, k * NI + (NI + DONE["w", GRP - 1]))
                        elif last_units(k) and u == 1:
                            pe.wait_ge(s_o, k * HB + HB)
                        else:
                            pe.wait_ge(s_add, k * WO_ALL + (WO_ALL + before - (1 if last_units(k) else 0)))
                        qs, ws = slice(u // 2 * P, (u // 2 + 1) * P), slice(u % 2 * CW, (u % 2 + 1) * CW)
                        for h in range(GRP):
                            last = split_matmul(nc, wo_bank(k, u), o_hi[:, h, qs], o_lo[:, h, qs],
                                                wo_hi[:, h, ws], wo_lo[:, h, ws], h == 0, h == GRP - 1)
                        last.then_inc(s_wo, 1)

            run(0)
            with pe.Fori(1, KVH) as k:
                run(k)
            run(KVH)

        @block.scalar
        def _(act):
            act.sem_inc(s_exp, BODY)
            act.sem_inc(s_on, HB)
            for i in range(SHARED):
                hi, lo, raw = split_operands(i)
                act.wait_ge(s_stage[i % 2], 16 * (i // 2 + 1))
                if ITEMS[i][0] == "k":
                    for c in range(NBLK):
                        nc.scalar.activation(hi[:, c * CW:(c + 1) * CW], raw[:, c * CW:(c + 1) * CW], ACT.Copy)\
                            .then_inc(s_khi, 1)
                    act.wait_ge(s_khi, NBLK)
                    act.sem_inc(s_hi, 1)
                    continue
                nc.scalar.activation(hi, raw, ACT.Copy).then_inc(s_hi, 1)

            def run(k):
                for s in slots(k):
                    if isinstance(k, int) and k == 0 and s == 2 * BLK:
                        act.dma_start(acc[:, :, :], x.rearrange("(t p) d -> p t d", p=P)).then_inc(s_acc, 16)
                    y = s - LAG_E
                    if exists(k, y):
                        n, i, c = y // BLK % HB, (y % BLK) // NBLK, y % NBLK
                        if y % BLK == 0:
                            pr_free = k * BODY + (BODY + (y // BLK - 1) * BLK)
                            act.wait_ge(s_tr, pr_free)
                        act.wait_ge(s_nm, k * TILES + (y // NBLK + 1))
                        nc.scalar.activation(pr[:, n % 2, i, c * CW:(c + 1) * CW], ps_s[:, y % RB, :], ACT.Exp,
                                             bias=nm[:, n % 2, i:i + 1],
                                             accum_out=rs[:, n % 2, i, c:c + 1]).then_inc(s_exp, 1)
                    y = s - LAG_O - 1
                    if y % BLK == 0 and exists(k, y):
                        h = y // BLK % GRP
                        if h == 0:
                            act.wait_ge(s_wo, k * WO_ALL + (WO_ALL + y // BLK // GRP * N_WO))
                        act.wait_ge(s_o, k * HB + (HB + y // BLK + 1))
                        nc.scalar.activation(o_hi[:, h, :], on[:, :], ACT.Copy).then_inc(s_ohi, 1)
                    y = s - LAG_RB - 1
                    if y % BLK == 0 and exists(k, y):
                        act.wait_ge(s_olo, k * HB + (HB + y // BLK))
                        act.wait_ge(s_rb, k * HB + (y // BLK + 1))
                        nc.scalar.activation(on[:, :], ps_m[:, :], ACT.Copy).then_inc(s_on, 1)
                    y = s - LAG_T
                    if exists(k, y):
                        j = y % BLK
                        act.wait_ge(s_pv, k * BODY + (BODY + y - 1))
                        act.wait_ge(s_tr, k * BODY + (BODY + y + 1))
                        nc.scalar.activation(pt_hi[:, j % 2, :], ps_p[:, j % 2, :], ACT.Copy).then_inc(s_phi, 1)

            run(0)
            with act.Fori(1, KVH) as k:
                run(k)
            run(KVH)

        @block.vector
        def _(dve):
            dve.sem_inc(s_plo, BODY)
            dve.sem_inc(s_o, HB)
            dve.sem_inc(s_olo, HB)
            dve.sem_inc(s_add, WO_ALL)
            for i in range(SHARED):
                hi, lo, raw = split_operands(i)
                if ITEMS[i][0] == "k":
                    for c in range(NBLK):
                        dve.wait_ge(s_khi, c + 1)
                        nc.vector.tensor_tensor(lo[:, c * CW:(c + 1) * CW], raw[:, c * CW:(c + 1) * CW],
                                                hi[:, c * CW:(c + 1) * CW].bitcast(F32), ALU.subtract)\
                            .then_inc(s_klo, 1)
                    dve.wait_ge(s_klo, NBLK)
                    dve.sem_inc(s_lo, 1)
                    continue
                dve.wait_ge(s_hi, i + 1)
                nc.vector.tensor_tensor(lo, raw, hi.bitcast(F32), ALU.subtract).then_inc(s_lo, 1)

            def run(k):
                for s in slots(k):
                    y = s - LAG_O
                    if y % BLK == 0 and exists(k, y):
                        dve.wait_ge(s_pv, k * BODY + (BODY + y + BLK))
                        dve.wait_ge(s_on, k * HB + (HB + y // BLK + 1))
                        nc.vector.tensor_tensor(on[:, :], ps_o[:, :], on[:, :], ALU.mult).then_inc(s_o, 1)
                    if exists(k, s):
                        n, i, c = s // BLK, (s % BLK) // NBLK, s % NBLK
                        dve.wait_ge(s_score, k * BODY + (BODY + s + 1))
                        nc.vector.reduce_max(mx[:, n % 2, i, c:c + 1], ps_s[:, s % RB, :], AX.X).then_inc(s_max, 1)
                        if c == NBLK - 1:
                            dve.wait_ge(s_max, k * BODY + s + 1)
                            nc.vector.tensor_reduce(nm[:, n % 2, i:i + 1], mx[:, n % 2, i, :], AX.X, ALU.max,
                                                    negate=True).then_inc(s_nm, 1)
                    y = s - LAG_T
                    if exists(k, y):
                        j = y % BLK
                        dve.wait_ge(s_phi, k * BODY + (y + 1))
                        nc.vector.tensor_tensor(pt_lo[:, j % 2, :], ps_p[:, j % 2, :], pt_hi[:, j % 2, :].bitcast(F32),
                                                ALU.subtract).then_inc(s_plo, 1)
                    y = s - LAG_RB + 2
                    if y % BLK == 0 and exists(k, y):
                        n = y // BLK % HB
                        dve.wait_ge(s_exp, k * BODY + (BODY + y + BLK))
                        nc.vector.tensor_reduce(rt[:, n % 2, :], rs[:, n % 2, :, :], AX.X, ALU.add).then_inc(s_rt, 1)
                    y = s - LAG_RB + 1
                    if y % BLK == 0 and exists(k, y):
                        n = y // BLK % HB
                        dve.wait_ge(s_rt, k * HB + (y // BLK + 1))
                        nc.vector.reciprocal(ri[:, n % 2, :], rt[:, n % 2, :]).then_inc(s_ri, 1)
                    y = s - LAG_O - 2
                    if y % BLK == 0 and exists(k, y):
                        h = y // BLK % GRP
                        dve.wait_ge(s_ohi, k * HB + (y // BLK + 1))
                        nc.vector.tensor_tensor(o_lo[:, h, :], on[:, :], o_hi[:, h, :].bitcast(F32),
                                                ALU.subtract).then_inc(s_olo, 1)
                    if s in WO_SLOTS and wo_exists(k, s):
                        b, u = WO_SLOTS[s]
                        if isinstance(k, int) and k == 0 and u == 0:
                            dve.wait_ge(s_acc, 16)
                        dve.wait_ge(s_wo, k * WO_ALL + (WO_ALL + u - b * N_WO + 1))
                        part = acc[:, b * QT + u // 2, u % 2 * CW:(u % 2 + 1) * CW]
                        nc.vector.tensor_tensor(part, part, wo_bank(k, u), ALU.add).then_inc(s_add, 1)

            run(0)
            with dve.Fori(1, KVH) as k:
                run(k)
            run(KVH)


def experts(nc, a_t, b_r, wr_t, acc, ident, stage_b, out):
    TOP = 8
    TAKEN = -3.0e38
    MC = KR // P
    RC = P // EXPERTS
    NE = D // CW
    NV = QT * NE

    with ExitStack() as ctx:
        def sb(name, shape, dt=F32):
            return ctx.enter_context(nc.sbuf_tensor(name, shape, dt))

        def sem(name):
            return ctx.enter_context(nc.semaphore(name))

        y_hi = sb("y_hi", [P, DC, SQ], F32R)
        y_lo = sb("y_lo", [P, DC, SQ], F32R)
        h_hi = sb("h_hi", [P, MC, SQ], F32R)
        h_lo = sb("h_lo", [P, MC, SQ], F32R)
        b_hi = sb("b_hi", [P, MC, D], F32R)
        b_lo = sb("b_lo", [P, MC, D], F32R)
        a_hi = sb("a_hi", [P, 2, DC, P], F32R)
        a_lo = sb("a_lo", [P, 2, DC, P], F32R)
        wr_hi = sb("wr_hi", [P, DC, EXPERTS], F32R)
        wr_lo = sb("wr_lo", [P, DC, EXPERTS], F32R)
        stage = stage_b[:, :, 0:D]
        yn = sb("yn", [P, 2, D])
        gx = sb("gx", [P, SQ])
        hg = stage_b[:, :, D:D + SQ]
        gates = sb("gates", [P, QT, P])
        ln_st = sb("ln_st_c", [P, NE, 6])
        ln_mv = sb("ln_mv_c", [P, 2])
        ln_r = sb("ln_r_c", [P, 2])
        z = sb("z", [P, 2, QT, EXPERTS])
        best = sb("best", [P, QT, 2, TOP])
        row = sb("row", [P, 4, QT])
        ps_x = ctx.enter_context(nc.psum_tensor("ps_xc", [P, NE, CW], F32))
        ps_h = ctx.enter_context(nc.psum_tensor("ps_h", [P, 2, SQ], F32))
        ps_y = ctx.enter_context(nc.psum_tensor("ps_y", [P, 2, CW], F32))
        ps_g = ctx.enter_context(nc.psum_tensor("ps_g", [P, SQ], F32))
        ps_r = ctx.enter_context(nc.psum_tensor("ps_r", [P, QT, EXPERTS], F32))

        s_stage = [sem("c_stage0"), sem("c_stage1")]
        s_hi = sem("c_hi")
        s_bhi = sem("c_bhi")
        s_lo = sem("c_lo")
        s_b = [sem("c_b0"), sem("c_b1")]
        s_blo = sem("c_blo")
        s_dv = sem("c_dv")
        s_var = sem("c_var")
        s_root = sem("c_root")
        s_yn = sem("c_yn")
        s_xtr = sem("c_xtr")
        s_xhi = sem("c_xhi")
        s_xlo = sem("c_xlo")
        s_r = sem("c_r")
        s_sc = sem("c_sc")
        s_rtr = sem("c_rtr")
        s_rmax = sem("c_rmax")
        s_e = sem("c_e")
        s_gate = sem("c_gate")
        s_h = sem("c_h")
        s_g = sem("c_g")
        s_gx = sem("c_gx")
        s_hg = sem("c_hg")
        s_hhi = sem("c_hhi")
        s_hlo = sem("c_hlo")
        s_y = sem("c_y")
        s_ot = sem("c_ot")
        s_out = sem("c_out")
        block = ctx.enter_context(nc.Block())

        ITEMS = [("r", 0, 0)] + [("a", b, m) for b in range(NB) for m in range(MC)]
        DONE = {it: i + 1 for i, it in enumerate(ITEMS)}

        LN_STEPS = ["n0", "n1", "t0", "n2", "t1", "n3", "t2", "t3", "r0", "s0"]
        STEPS = [(s[0], 0, int(s[1])) for s in LN_STEPS]
        STEPS += [("h", 0, m) for m in range(MC + 1)]
        between = [["n0"], ["n1", "t0"], ["n2", "t1"], ["n3", "t2"], ["t3", "r0"], ["s0"], [], []]
        for v in range(NV):
            STEPS += [("y", 0, v)] + [(s[0], 1, int(s[1])) for s in between[v]]
        STEPS += [("h", 1, m) for m in range(MC + 1)] + [("y", 1, v) for v in range(NV)]

        @block.sync
        def _(sp):
            a_view = a_t.rearrange("(j p) n -> p j n", p=P)
            for i, (kind, b, m) in enumerate(ITEMS):
                if i >= 2:
                    sp.wait_ge(s_lo, i - 1)
                if kind == "r":
                    dst = stage[:, i % 2, 0:DC * EXPERTS].rearrange("p (j n) -> p j n", j=DC)
                    src = wr_t.rearrange("(j p) n -> p j n", p=P)
                else:
                    dst = stage[:, i % 2, :].rearrange("p (j n) -> p j n", j=DC)
                    src = a_view[:, :, m * P:(m + 1) * P]
                sp.dma_start(dst, src).then_inc(s_stage[i % 2], 16)
                if 2 <= i < 2 + MC:
                    m = i - 2
                    if m < 2:
                        sp.wait_ge(s_xtr, NE * (QT - 1 + m))
                    else:
                        sp.wait_ge(s_blo, m - 1)
                    sp.dma_start(yn[:, m % 2, :], b_r[m * P:(m + 1) * P, :]).then_inc(s_b[m % 2], 16)

        @block.gpsimd
        def _(pool):
            for i, (kind, b, m) in enumerate(ITEMS):
                pool.wait_ge(s_stage[i % 2], 16 * (i // 2 + 1))
                if kind == "r":
                    hi, lo, raw = wr_hi[:, :, :], wr_lo[:, :, :], stage[:, i % 2, 0:DC * EXPERTS]
                else:
                    hi, lo, raw = a_hi[:, m % 2, :, :], a_lo[:, m % 2, :, :], stage[:, i % 2, :]
                    if b * MC + m >= 2:
                        pool.wait_ge(s_h, b * MC + m - 1)
                hi, lo = hi.rearrange("p j n -> p (j n)"), lo.rearrange("p j n -> p (j n)")
                nc.gpsimd.tensor_scalar(hi, raw, 1.0, 1.0, ALU.mult, ALU.mult).then_inc(s_hi, 1)
                pool.wait_ge(s_hi, i + 1)
                nc.gpsimd.tensor_tensor(lo, raw, hi.bitcast(F32), ALU.subtract).then_inc(s_lo, 1)

        @block.tensor
        def _(pe):
            for kind, b, n in STEPS:
                if kind == "t":
                    t = b * QT + n
                    pe.wait_ge(s_yn, t + 1)
                    for e in range(NE):
                        if t:
                            pe.wait_ge(s_xlo, NE * (t - 1) + e + 1)
                        for j in range(HPC):
                            c = e * HPC + j
                            last = nc.tensor.transpose(ps_x[:, e, j * P:(j + 1) * P],
                                                       yn[:, t % 2, c * P:(c + 1) * P], ident[:, :])
                        last.then_inc(s_xtr, 1)
                elif kind == "r":
                    if b == 0:
                        pe.wait_ge(s_lo, DONE["r", 0, 0])
                    pe.wait_ge(s_xlo, NE * QT * (b + 1))
                    if b:
                        pe.wait_ge(s_gx, b)
                    for j in range(DC):
                        last = split_matmul(nc, ps_g[0:EXPERTS, :], wr_hi[:, j, :], wr_lo[:, j, :],
                                            y_hi[:, j, :], y_lo[:, j, :], j == 0, j == DC - 1)
                    last.then_inc(s_r, 1)
                elif kind == "s":
                    pe.wait_ge(s_sc, b + 1)
                    if b:
                        pe.wait_ge(s_gate, RC * b)
                    for i in range(QT):
                        last = nc.tensor.transpose(ps_r[:, i, :], gx[0:EXPERTS, i * P:(i + 1) * P],
                                                   ident[0:EXPERTS, 0:EXPERTS])
                    last.then_inc(s_rtr, 1)
                elif kind == "h":
                    if n == MC:
                        continue
                    q = b * MC + n
                    pe.wait_ge(s_lo, DONE["a", b, n])
                    if q >= 2:
                        pe.wait_ge(s_hg, q - 1)
                    for j in range(DC):
                        if n == 1 and j == DC - 2:
                            pe.wait_ge(s_gate, RC * (b + 1))
                            for i in range(QT):
                                last = nc.tensor.transpose(ps_g[:, i * P:(i + 1) * P], gates[:, i, :], ident[:, :])
                            last.then_inc(s_g, 1)
                        last = split_matmul(nc, ps_h[:, n % 2, :], a_hi[:, n % 2, j, :], a_lo[:, n % 2, j, :],
                                            y_hi[:, j, :], y_lo[:, j, :], j == 0, j == DC - 1)
                    last.then_inc(s_h, 1)
                elif kind == "y":
                    q = b * NV + n
                    i, e = n // NE, n % NE
                    if q >= 2:
                        pe.wait_ge(s_ot, q - 1)
                    rows, cols = slice(i * P, (i + 1) * P), slice(e * CW, (e + 1) * CW)
                    for m in range(MC):
                        if n == 0:
                            pe.wait_ge(s_hlo, MC * b + m + 1)
                            if b == 0:
                                pe.wait_ge(s_blo, m + 1)
                        last = split_matmul(nc, ps_y[:, n % 2, :], h_hi[:, m, rows], h_lo[:, m, rows],
                                            b_hi[:, m, cols], b_lo[:, m, cols], m == 0, m == MC - 1)
                    last.then_inc(s_y, 1)

        @block.scalar
        def _(act):
            for kind, b, n in STEPS:
                t = b * QT + n
                if kind == "n":
                    act.wait_ge(s_var, t + 1)
                    nc.scalar.activation(ln_r[:, 0:1], ln_mv[:, 1:2], ACT.Sqrt).then_inc(s_root, 1)
                elif kind == "t":
                    if b == 1 and n == 0:
                        act.wait_ge(s_h, MC)
                    for e in range(NE):
                        act.wait_ge(s_xtr, NE * t + e + 1)
                        nc.scalar.activation(y_hi[:, e * HPC:(e + 1) * HPC, n * P:(n + 1) * P],
                                             ps_x[:, e, :].rearrange("p (j t) -> p j t", j=HPC), ACT.Copy)\
                            .then_inc(s_xhi, 1)
                elif kind == "r":
                    act.wait_ge(s_r, b + 1)
                    if b:
                        act.wait_ge(s_hg, MC * b)
                    nc.scalar.activation(gx[0:EXPERTS, :], ps_g[0:EXPERTS, :], ACT.Copy).then_inc(s_sc, 1)
                elif kind == "s":
                    act.wait_ge(s_rmax, b + 1)
                    for i in range(QT):
                        nc.scalar.activation(z[:, 1, i, :], gates[:, i, 0:EXPERTS], ACT.Exp, bias=row[:, 0, i:i + 1])\
                            .then_inc(s_e, 1)
                elif kind == "h":
                    if n > 0:
                        m = n - 1
                        q = b * MC + m
                        if m == 0:
                            act.wait_ge(s_g, b + 1)
                            if b:
                                act.wait_ge(s_hg, MC)
                            nc.scalar.activation(gx[:, :], ps_g[:, :], ACT.Copy).then_inc(s_gx, 1)
                        if b == 1 and m == 0:
                            act.wait_ge(s_y, NV)
                        act.wait_ge(s_hg, q + 1)
                        nc.scalar.activation(h_hi[:, m, :], hg[:, m % 2, :], ACT.Copy).then_inc(s_hhi, 1)
                        if b == 0:
                            act.wait_ge(s_b[m % 2], 16 * (m // 2 + 1))
                            nc.scalar.activation(b_hi[:, m, :], yn[:, m % 2, :], ACT.Copy)\
                                .then_inc(s_bhi, 1)
                elif kind == "y":
                    q = b * NV + n
                    act.wait_ge(s_ot, q + 1)
                    act.dma_start(out[(b * QT + n // NE) * P:(b * QT + n // NE + 1) * P,
                                      n % NE * CW:(n % NE + 1) * CW],
                                  acc[:, b * QT + n // NE, n % NE * CW:(n % NE + 1) * CW]).then_inc(s_out, 16)
            act.wait_ge(s_out, 16 * NB * NV)

        @block.vector
        def _(dve):
            links = [0]

            def link(ins):
                links[0] += 1
                ins.then_inc(s_dv, 1)
                dve.wait_ge(s_dv, links[0])

            for kind, b, n in STEPS:
                t = b * QT + n
                if kind == "n":
                    for e in range(NE):
                        ins = nc.vector.bn_stats(ln_st[:, e, :], acc[:, t, e * CW:(e + 1) * CW])
                        if e == NE - 1:
                            link(ins)
                    link(nc.vector.bn_aggr(ln_mv[:, :], ln_st[:, :, :]))
                    nc.vector.tensor_scalar(ln_mv[:, 1:2], ln_mv[:, 1:2], LN_EPS, None, ALU.add).then_inc(s_var, 1)
                    dve.wait_ge(s_root, t + 1)
                    link(nc.vector.reciprocal(ln_r[:, 1:2], ln_r[:, 0:1]))
                    if t >= 2:
                        dve.wait_ge(s_xtr, NE * (t - 1))
                    if t == QT:
                        dve.wait_ge(s_blo, MC)
                    nc.vector.tensor_scalar(yn[:, t % 2, :], acc[:, t, :], ln_mv[:, 0:1], ln_r[:, 1:2],
                                            ALU.subtract, ALU.mult).then_inc(s_yn, 1)
                    dve.wait_ge(s_yn, t + 1)
                elif kind == "t":
                    for e in range(NE):
                        dve.wait_ge(s_xhi, NE * t + e + 1)
                        rows, cols = slice(e * HPC, (e + 1) * HPC), slice(n * P, (n + 1) * P)
                        nc.vector.tensor_tensor(y_lo[:, rows, cols], ps_x[:, e, :].rearrange("p (j t) -> p j t", j=HPC),
                                                y_hi[:, rows, cols].bitcast(F32), ALU.subtract).then_inc(s_xlo, 1)
                elif kind == "s":
                    scores = gates[:, :, 0:EXPERTS]
                    dve.wait_ge(s_rtr, b + 1)
                    if b:
                        dve.wait_ge(s_g, b)
                    link(nc.vector.tensor_copy(scores, ps_r[:, :, :]))
                    for i in range(QT):
                        ins = nc.vector.max(best[:, i, 0, :], scores[:, i, :])
                    link(ins)
                    nc.vector.tensor_scalar(row[:, 0, :], best[:, :, 0, 0], -1.0, None, ALU.mult).then_inc(s_rmax, 1)
                    for i in range(QT):
                        ins = nc.vector.match_replace(z[:, 0, i, :], best[:, i, 0, :], scores[:, i, :], TAKEN)
                    link(ins)
                    for i in range(QT):
                        ins = nc.vector.max(best[:, i, 1, :], z[:, 0, i, :])
                    link(ins)
                    dve.wait_ge(s_e, QT * (b + 1))
                    for i in range(QT):
                        ins = nc.vector.match_replace(scores[:, i, :], best[:, i, 1, :], z[:, 0, i, :], TAKEN)
                    link(ins)
                    link(nc.vector.tensor_scalar(z[:, 0, :, :], scores, TAKEN, None, ALU.is_equal))
                    link(nc.vector.tensor_tensor(z[:, 1, :, :], z[:, 1, :, :], z[:, 0, :, :], ALU.mult))
                    link(nc.vector.tensor_reduce(row[:, 1, :], z[:, 1, :, :], AX.X, ALU.add))
                    link(nc.vector.reciprocal(row[:, 2, :], row[:, 1, :]))
                    link(nc.vector.tensor_scalar(row[:, 3, :], row[:, 2, :], GATE_SCALE, None, ALU.mult))
                    for r in range(RC):
                        nc.vector.tensor_tensor(gates[:, :, r * EXPERTS:(r + 1) * EXPERTS], z[:, 1, :, :],
                                                row[:, 3, :].rearrange("p (t a) -> p t a", a=1)
                                                .to_broadcast([P, QT, EXPERTS]), ALU.mult).then_inc(s_gate, 1)
                elif kind == "h":
                    if n > 0:
                        m = n - 1
                        q = b * MC + m
                        dve.wait_ge(s_h, q + 1)
                        dve.wait_ge(s_gx, b + 1)
                        if q >= 2:
                            dve.wait_ge(s_hlo, q - 1)
                        nc.vector.tensor_tensor(hg[:, m % 2, :], ps_h[:, m % 2, :], gx[:, :], ALU.mult)\
                            .then_inc(s_hg, 1)
                        dve.wait_ge(s_hhi, q + 1)
                        nc.vector.tensor_tensor(h_lo[:, m, :], hg[:, m % 2, :], h_hi[:, m, :].bitcast(F32),
                                                ALU.subtract).then_inc(s_hlo, 1)
                        if b == 0:
                            dve.wait_ge(s_bhi, m + 1)
                            nc.vector.tensor_tensor(b_lo[:, m, :], yn[:, m % 2, :],
                                                    b_hi[:, m, :].bitcast(F32), ALU.subtract).then_inc(s_blo, 1)
                elif kind == "y":
                    q = b * NV + n
                    dve.wait_ge(s_y, q + 1)
                    part = acc[:, b * QT + n // NE, n % NE * CW:(n % NE + 1) * CW]
                    nc.vector.tensor_tensor(part, part, ps_y[:, n % 2, :], ALU.add).then_inc(s_ot, 1)


def cross_attention_and_experts(nc, x, ctx_t, w_kvq, q_norm, k_norm, wo, a_t, b_r, wr_t, out):
    x_rows = x.rearrange("b s d -> (b s) d")
    out_rows = out.rearrange("b s d -> (b s) d")
    k_s = nc.dram_tensor("k_s", (KVH, NB, P, SK), F32, kind="Internal").ap()
    v_s = nc.dram_tensor("v_s", (KVH, NB, P, KT, DH), F32, kind="Internal").ap()
    q_s = nc.dram_tensor("q_s", (HEADS, NB, P, SQ), F32, kind="Internal").ap()
    with (nc.sbuf_tensor("ident", [P, P], F32) as ident, nc.semaphore("b_stage0") as s_stage0,
          nc.semaphore("b_stage1") as s_stage1):
        with nc.sbuf_tensor("stage_b", [P, 2, SK], F32) as stage:
            projections(nc, x_rows, ctx_t, w_kvq, q_norm, k_norm, ident, stage, [s_stage0, s_stage1], k_s, v_s, q_s)
            with nc.sbuf_tensor("acc", [P, NB * QT, D], F32) as acc:
                attention(nc, k_s, v_s, q_s, wo, x_rows, acc, ident, stage, [s_stage0, s_stage1])
                experts(nc, a_t, b_r, wr_t, acc, ident, stage, out_rows)


def kernel(**inputs):
    import numpy as np
    import concourse.bacc as bacc
    from concourse.bass_utils import run_bass_kernel_spmd as run

    nc = bacc.Bacc("TRN2", target_bir_lowering=False, num_devices=1)
    g = {k: np.asarray(v) for k, v in inputs.items()}
    arrays = {
        "in_x": np.ascontiguousarray(g["x"]),
        "in_ctx_t": np.ascontiguousarray(g["ctx_4096"].transpose(0, 2, 1)),
        "in_w_kvq": np.concatenate([g["L0_xattn_Wk"], g["L0_xattn_Wv"], g["L0_xattn_Wq"]], axis=1),
        "in_q_norm": g["L0_xattn_q_norm_w"],
        "in_k_norm": g["L0_xattn_k_norm_w"],
        "in_wo": g["L0_xattn_Wo"],
        "in_a_t": np.ascontiguousarray(g["L0_ffn_A"].transpose(2, 1, 0).reshape(D, KR)),
        "in_b_r": np.ascontiguousarray(g["L0_ffn_B"].transpose(2, 0, 1).reshape(KR, D)),
        "in_wr_t": np.ascontiguousarray(g["L0_ffn_Wr"].T),
    }
    ins = [nc.dram_tensor(n, a.shape, F32, kind="ExternalInput").ap() for n, a in arrays.items()]
    out = nc.dram_tensor("out_0", (NB, SQ, D), F32, kind="ExternalOutput").ap()
    cross_attention_and_experts(nc, *ins, out)
    r = run(nc, [arrays], core_ids=[0])
    return r.results[0]["out_0"]
```
